# Optimizing a Trainium2 kernel written in Bass

```python
import numpy as np
import jax
import jax.numpy as jnp

def _softmax(x, axis=-1):
    return jax.nn.softmax(x, axis=axis)

def _gelu(x):
    return jax.nn.gelu(x, approximate=True)

def _silu(x):
    return jax.nn.silu(x)

def _sigmoid(x):
    return jax.nn.sigmoid(x)

def _layernorm(x, axis=-1, eps=1e-05):
    m = jnp.mean(x, axis=axis, keepdims=True)
    v = jnp.var(x, axis=axis, keepdims=True)
    return (x - m) / jnp.sqrt(v + eps)

def _scatter_add(tgt, idx, src, axis=0):
    return tgt.at[idx].add(src)

def _segment_sum(src, seg, n):
    return jax.ops.segment_sum(src, seg, n)
kernel_name = 'mk_conv_preact_d1_conv_nchw128_r4_14a504'

def setup_inputs(seed: int=0):
    np.random.seed(seed)
    _w = jnp.asarray

    def _rec_inputs():
        import jax
        import jax.numpy as jnp
        _gk = jax.random.key(seed)
        x = -0.0003957 + 1 * jax.random.normal(jax.random.fold_in(_gk, 1), (32, 32, 56, 56), jnp.float32)
        return x
    x = _rec_inputs()

    def _L0_conv_setup():
        import jax, jax.numpy as jnp
        import numpy as np
        DILATED_KS = (7, 7)
        SCALING = 1.0
        GROUPS = 1
        STRIDE = (1, 1)
        PADDING = (3, 3)

        def construct_kernel(weight, P):
            Hk, Wk = DILATED_KS
            lim_h, lim_w = (Hk // 2, Wk // 2)
            O, Cg, K = weight.shape
            ph = jnp.clip(P[0] * SCALING, -lim_h, lim_h) + lim_h
            pw = jnp.clip(P[1] * SCALING, -lim_w, lim_w) + lim_w
            ih = jnp.floor(ph).astype(jnp.int32)
            iw = jnp.floor(pw).astype(jnp.int32)
            rh = ph - ih
            rw = pw - iw
            cidx = jnp.broadcast_to(jnp.arange(Cg)[:, None], (Cg, K))
            kern = jnp.zeros((O, Cg, Hk, Wk), dtype=weight.dtype)
            corners = [(0, 0, (1 - rh) * (1 - rw)), (0, 1, (1 - rh) * rw), (1, 0, rh * (1 - rw)), (1, 1, rh * rw)]
            for di, dj, frac in corners:
                kern = kern.at[:, cidx, ih + di, iw + dj].add(weight * frac[None], mode='drop')
            return kern
        key = jax.random.key(seed)
        k1, k2, k3, k4 = jax.random.split(key, 4)
        x = jax.random.normal(k1, (32, 32, 56, 56), dtype=jnp.float32)
        weight = jax.random.normal(k2, (32, 32, 9), dtype=jnp.float32) * 0.05
        P = jax.random.normal(k3, (2, 32, 9), dtype=jnp.float32)
        bias = jax.random.normal(k4, (32,), dtype=jnp.float32) * 0.05
        return {'x': x, 'weight': weight, 'P': P, 'bias': bias}
    _L0_conv_all = _L0_conv_setup()
    _L0_conv_in = {k: v for k, v in _L0_conv_all.items() if k in ('weight', 'P', 'bias')}
    del _L0_conv_all
    return {'x': x, 'L0_conv_weight': _L0_conv_in['weight'], 'L0_conv_P': _L0_conv_in['P'], 'L0_conv_bias': _L0_conv_in['bias']}

def reference(x, L0_conv_weight, L0_conv_P, L0_conv_bias):
    import jax
    import jax.numpy as jnp

    def _L0_conv_ref(x, weight, P, bias):
        import jax, jax.numpy as jnp
        import numpy as np
        DILATED_KS = (7, 7)
        SCALING = 1.0
        GROUPS = 1
        STRIDE = (1, 1)
        PADDING = (3, 3)

        def construct_kernel(weight, P):
            Hk, Wk = DILATED_KS
            lim_h, lim_w = (Hk // 2, Wk // 2)
            O, Cg, K = weight.shape
            ph = jnp.clip(P[0] * SCALING, -lim_h, lim_h) + lim_h
            pw = jnp.clip(P[1] * SCALING, -lim_w, lim_w) + lim_w
            ih = jnp.floor(ph).astype(jnp.int32)
            iw = jnp.floor(pw).astype(jnp.int32)
            rh = ph - ih
            rw = pw - iw
            cidx = jnp.broadcast_to(jnp.arange(Cg)[:, None], (Cg, K))
            kern = jnp.zeros((O, Cg, Hk, Wk), dtype=weight.dtype)
            corners = [(0, 0, (1 - rh) * (1 - rw)), (0, 1, (1 - rh) * rw), (1, 0, rh * (1 - rw)), (1, 1, rh * rw)]
            for di, dj, frac in corners:
                kern = kern.at[:, cidx, ih + di, iw + dj].add(weight * frac[None], mode='drop')
            return kern
        kern = construct_kernel(weight, P)
        out = jax.lax.conv_general_dilated(x, kern, window_strides=STRIDE, padding=[(PADDING[0], PADDING[0]), (PADDING[1], PADDING[1])], dimension_numbers=('NCHW', 'OIHW', 'NCHW'), feature_group_count=GROUPS)
        return out + bias[None, :, None, None]

    def _gn(v, G=32, eps=1e-05):
        B_, C_, H_, W_ = v.shape
        g = v.reshape(B_, G, C_ // G, H_, W_)
        m = jnp.mean(g, axis=(2, 3, 4), keepdims=True)
        s = jnp.var(g, axis=(2, 3, 4), keepdims=True)
        return ((g - m) / jnp.sqrt(s + eps)).reshape(v.shape)

    def _ln_c(v, eps=1e-06):
        m = jnp.mean(v, axis=1, keepdims=True)
        s = jnp.var(v, axis=1, keepdims=True)
        return (v - m) / jnp.sqrt(s + eps)

    def _ln_t(v, eps=1e-05):
        m = jnp.mean(v, axis=-1, keepdims=True)
        s = jnp.var(v, axis=-1, keepdims=True)
        return (v - m) / jnp.sqrt(s + eps)

    def _to_tokens(v):
        B_, C_, H_, W_ = v.shape
        return v.reshape(B_, C_, H_ * W_).transpose(0, 2, 1)

    def _from_tokens(t, like):
        B_, C_, H_, W_ = like.shape
        return t.transpose(0, 2, 1).reshape(B_, C_, H_, W_)
    x = x + _L0_conv_ref(_gn(x), L0_conv_weight, L0_conv_P, L0_conv_bias)
    return x

_drawn_inputs = setup_inputs


def setup_inputs(seed=0):
    import zlib

    import numpy as np

    out = dict(_drawn_inputs(seed))
    spreads = {}
    factors = {}
    for name, (base, spread) in spreads.items():
        noise = np.random.default_rng([zlib.crc32(name.encode()), seed]).standard_normal(out[name].shape)
        drawn = base * np.exp(spread * noise) if base else spread * noise
        out[name] = jnp.asarray(drawn.astype(out[name].dtype))
    for name, factor in factors.items():
        out[name] = (out[name] * factor).astype(out[name].dtype)
    return out
```

```python
import concourse.bass as bass
from concourse import mybir
from contextlib import ExitStack

BATCH, CH, SIDE = 32, 32, 56
TAPS = 7
POINTS = 9
GROUPS = 4
ROWS = SIDE // GROUPS
PER = 2
UNITS = BATCH // PER
LINES = PER * ROWS
PLANE = ROWS * SIDE
PAD = TAPS // 2
WPAD = 64
QW = SIDE // 4
QS = QW + 1
QP = 16
N = LINES * QW
V = 12
VO = V * CH
X_SCALE = 256.0
W_SCALE = 2048.0
EPS = 1e-5
RING = 4
BANKS = 6
STREAMS = [(1, 0), (1, 1), (1, 2), (0, 0), (0, 1), (0, 2), (2, 0), (2, 1), (2, 2)]
NS = len(STREAMS)
STEP_OF = [3, 2, 4, 6, 5, 7, 9, 8, 10]
PREP = 10
NEWTON = 5
DMA = 16
SETUP = GROUPS * DMA
LOAD = PER * GROUPS * DMA


def build(nc, x, weight, P, bias, out):
    fp32 = mybir.dt.float32
    fp16 = mybir.dt.float16
    i32 = mybir.dt.int32
    ALU = mybir.AluOpType
    ACT = mybir.ActivationFunctionType
    AX = mybir.AxisListType

    ctx = ExitStack()
    with ctx:
        def sb(name, shape, dt):
            return ctx.enter_context(nc.sbuf_tensor(name, shape, dt))

        def sem(name):
            return ctx.enter_context(nc.semaphore(name))

        xraw = sb("xraw", [128, RING * PER, PLANE], fp32)
        junk = sb("junk", [128, PER, PLANE], fp16)
        xn = sb("xn", [128, LINES, WPAD], fp32)
        d = sb("d", [128, 2, LINES, WPAD // 2], fp32)
        e = sb("e", [128, 3, 2, LINES, QP], fp32)
        xhi = sb("xhi", [128, 2, NS, PER, ROWS + 2, QP], fp16)
        xlo = sb("xlo", [128, 2, NS, PER, ROWS + 2, QP], fp16)
        late = sb("late", [128, 9 * N + PER * PLANE], fp32)
        middle = late[:, 0:3 * N].rearrange("p (j n) -> p j n", j=3)
        pair = late[:, 3 * N:9 * N].rearrange("p (j n) -> p j n", j=6)
        conv = late[:, 9 * N:9 * N + PER * PLANE]
        prod = late[:, 0:2 * TAPS * CH * POINTS].rearrange("p (a o k) -> p a o k", o=CH, k=POINTS)
        result = sb("result", [128, 2, PER * PLANE], fp32)
        fold = sb("fold", [128, 128], fp32)
        xsum = sb("xsum", [128, PER], fp32)
        negmean = sb("negmean", [128, PER], fp32)
        ssq = sb("ssq", [128, PER], fp32)
        var = sb("var", [128, PER], fp32)
        std = sb("std", [128, PER], fp32)
        rinv = sb("rinv", [128, PER], fp32)
        rtmp = sb("rtmp", [128, PER], fp32)
        scale = sb("scale", [128, PER], fp32)
        ident = sb("ident", [128, 128], fp32)
        ones = sb("ones", [1, 128], fp32)
        pts = sb("pts", [128, 2, POINTS], fp32)
        wts = sb("wts", [128, CH, POINTS], fp32)
        coloff = sb("coloff", [128, 2], fp32)
        hath = sb("hath", [128, TAPS, POINTS], fp32)
        hatw = sb("hatw", [128, 2, POINTS], fp32)
        hat2 = sb("hat2", [128, 2, TAPS, POINTS], fp32)
        kern = sb("kern", [128, 2, TAPS * CH], fp32)
        filt = sb("filt", [128, 3, 4, VO], fp32)
        filtsum = result[:, :, :].rearrange("p a n -> p (a n)")[:, 0:6 * VO].rearrange(
            "p (i q v) -> p i q v", i=3, q=2)
        whi = sb("whi", [128, 3, 3, 2, VO], fp16)
        wlo = sb("wlo", [128, 3, 3, 2, VO], fp16)
        wmax = sb("wmax", [128, 1], fp32)
        srow = sb("srow", [1, 4], fp32)
        scales = sb("scales", [128, 2], fp32)
        biascol = sb("biascol", [128, 1], fp32)

        banks = [ctx.enter_context(nc.psum_tensor(f"bank{k}", [128, 512], fp32)) for k in range(BANKS)]
        mean_ps = ctx.enter_context(nc.psum_tensor("mean_ps", [128, 512], fp32))
        var_ps = ctx.enter_context(nc.psum_tensor("var_ps", [128, 512], fp32))

        x_loaded = [sem("x_loaded_even"), sem("x_loaded_odd")]
        stored = [sem("stored_even"), sem("stored_odd")]
        points_loaded = sem("points_loaded")
        weights_loaded = sem("weights_loaded")
        bias_loaded = sem("bias_loaded")
        kernel_spread = sem("kernel_spread")
        sum_ready = sem("sum_ready")
        mean_in_psum = sem("mean_in_psum")
        negmean_ready = sem("negmean_ready")
        ssq_ready = sem("ssq_ready")
        var_in_psum = sem("var_in_psum")
        var_ready = sem("var_ready")
        std_ready = sem("std_ready")
        newton = sem("newton")
        prepared = sem("prepared")
        hi_ready = sem("hi_ready")
        lo_ready = sem("lo_ready")
        conv_done = sem("conv_done")
        middle_ready = sem("middle_ready")
        pair_ready = sem("pair_ready")
        conv_summed = sem("conv_summed")
        result_ready = sem("result_ready")
        fold_built = sem("fold_built")
        ident_built = sem("ident_built")
        ones_built = sem("ones_built")
        coloff_built = sem("coloff_built")
        filt_zeroed = sem("filt_zeroed")
        pads_zeroed = sem("pads_zeroed")
        xn_zeroed = sem("xn_zeroed")
        hats = sem("hats")
        wmax_ready = sem("wmax_ready")
        wmax_row = sem("wmax_row")
        srow_step = sem("srow_step")
        scales_in_psum = sem("scales_in_psum")
        scales_ready = sem("scales_ready")
        kern_ready = sem("kern_ready")
        filt_summed = sem("filt_summed")
        whi_ready = sem("whi_ready")
        wlo_ready = sem("wlo_ready")

        block = ctx.enter_context(nc.Block())

        def image(r, m):
            return xraw[:, r * PER + m, :]

        def dram_rows(t, u, m, g):
            return t[bass.ds(u * PER + m, 1), :, g::GROUPS, :].rearrange("m c n w -> (m c) n w")

        def stream(s):
            i, j = STREAMS[s]
            if j != 1:
                return e[:, i, j // 2, :, 0:QS]
            if i == 1:
                return xn[:, :, 3:3 + 4 * QS:4]
            return d[:, i // 2, :, 1:1 + 2 * QS:2]

        def split(t, par, s):
            return t[:, par, s, :, 1:1 + ROWS, 0:QS]

        def as_images(ap):
            return ap.rearrange("p (m n) w -> p m n w", m=PER)

        def filter_of(i, j):
            return filtsum[:, i, :, :] if j == 1 else filt[:, i, j // 2::2, :]

        def scaled(t, i, j):
            return t[:, i, j, :, :]

        @block.sync
        def _(sp):
            def load(u, r):
                for m in range(PER):
                    for g in range(GROUPS):
                        sp.dma_start(image(r, m)[32 * g:32 * g + 32, :].rearrange("c (n w) -> c n w", w=SIDE),
                                     dram_rows(x, u, m, g)).then_inc(x_loaded[r % 2], DMA)

            def store(u, par):
                for m in range(PER):
                    for g in range(GROUPS):
                        sp.dma_start(dram_rows(out, u, m, g),
                                     result[32 * g:32 * g + 32, par, PLANE * m:PLANE * (m + 1)].rearrange(
                                         "c (n w) -> c n w", w=SIDE)).then_inc(stored[par], DMA)

            load(0, 0)
            load(1, 1)
            sp.wait_ge(sum_ready, 1)
            load(2, 2)
            sp.wait_ge(sum_ready, 2)
            load(3, 3)
            with sp.Fori(0, UNITS // RING - 1) as it:
                for h in range(RING):
                    u = it * RING + h
                    sp.wait_ge(result_ready, u + 1)
                    store(u, h % 2)
                    sp.wait_ge(sum_ready, u + 3)
                    load(u + RING, h)
            for u in range(UNITS - RING, UNITS):
                sp.wait_ge(result_ready, u + 1)
                store(u, u % 2)
            for par in range(2):
                sp.wait_ge(stored[par], LOAD * (UNITS // 2))

        @block.scalar
        def _(act):
            for g in range(GROUPS):
                act.dma_start(pts[32 * g:32 * g + 32, :, :], P.rearrange("t c k -> c t k")).then_inc(points_loaded, DMA)
            for g in range(GROUPS):
                act.dma_start(wts[32 * g:32 * g + 32, :, :],
                              weight.rearrange("o c k -> c o k")).then_inc(weights_loaded, DMA)
            for g in range(GROUPS):
                act.dma_start(biascol[32 * g:32 * g + 32, :],
                              bias.rearrange("(c a) -> c a", a=1)).then_inc(bias_loaded, DMA)

            def sums(u, r, nth):
                act.wait_ge(x_loaded[r % 2], LOAD * (nth + 1))
                act.wait_ge(mean_in_psum, u)
                for m in range(PER):
                    last = act.activation(junk[:, m, :], image(r, m), ACT.Identity, accum_out=xsum[:, m:m + 1])
                last.then_inc(sum_ready, 1)

            def squares(u, r):
                act.wait_ge(negmean_ready, u + 1)
                for m in range(PER):
                    last = act.activation(junk[:, m, :], image(r, m), ACT.Square, bias=negmean[:, m:m + 1],
                                          accum_out=ssq[:, m:m + 1])
                last.then_inc(ssq_ready, 1)

            def root(u):
                act.wait_ge(var_ready, u + 1)
                act.activation(std[:, :], var[:, :], ACT.Sqrt).then_inc(std_ready, 1)

            def high(u, par, s):
                act.wait_ge(prepared, PREP * u + STEP_OF[s])
                act.activation(split(xhi, par, s), as_images(stream(s)), ACT.Copy).then_inc(hi_ready, 1)

            def step(u, h, nth, streams, stats):
                def mid(j):
                    act.wait_ge(conv_done, NS * u + j + 1)
                    act.wait_ge(pair_ready, 6 * u + 4 + j)
                    act.activation(middle[:, j, :], banks[(NS * h + j) % BANKS][:, 0:N], ACT.Identity,
                                   bias=biascol[:, 0:1] if j == 1 else 0.0,
                                   scale=scales[:, 1:2]).then_inc(middle_ready, 1)
                if stats:
                    sums(u + 2, (h + 2) % RING, nth)
                for j in range(3):
                    mid(j)
                    if streams:
                        for s in range(3 * j, 3 * j + 3):
                            high(u + 1, 1 - h % 2, s)
                if stats:
                    squares(u + 2, (h + 2) % RING)
                    root(u + 2)

            sums(0, 0, 0)
            squares(0, 0)
            root(0)
            act.wait_ge(pads_zeroed, 2)
            for s in range(NS):
                high(0, 0, s)
            sums(1, 1, 0)
            squares(1, 1)
            root(1)
            act.wait_ge(scales_ready, 1)
            for n, (i, j) in enumerate(STREAMS):
                if n == 0:
                    act.wait_ge(filt_summed, 2)
                act.activation(scaled(whi, i, j), filter_of(i, j), ACT.Copy, scale=scales[:, 0:1]
                               ).then_inc(whi_ready, 1)
            act.wait_ge(bias_loaded, SETUP)
            with act.Fori(0, UNITS // RING - 1) as it:
                for h in range(RING):
                    step(it * RING + h, h, it * (RING // 2) + (h // 2 + 1), True, True)
            for h in range(RING):
                u = UNITS - RING + h
                step(u, h, u // 2 + 1, u + 1 < UNITS, u + 2 < UNITS)

        @block.vector
        def _(dve):
            def mean(u):
                dve.wait_ge(mean_in_psum, u + 1)
                dve.tensor_copy(negmean[:, :], mean_ps[:, 0:PER]).then_inc(negmean_ready, 1)

            def rstd(u):
                dve.wait_ge(var_in_psum, u + 1)
                dve.tensor_scalar(var[:, :], var_ps[:, 0:PER], -1.0, EPS, ALU.mult, ALU.add).then_inc(var_ready, 1)
                dve.wait_ge(std_ready, u + 1)
                k = NEWTON * u
                dve.reciprocal(rinv[:, :], std[:, :]).then_inc(newton, 1)
                dve.wait_ge(newton, k + 1)
                dve.tensor_tensor(rtmp[:, :], rinv[:, :], rinv[:, :], ALU.mult).then_inc(newton, 1)
                dve.wait_ge(newton, k + 2)
                dve.tensor_tensor(rtmp[:, :], rtmp[:, :], var[:, :], ALU.mult).then_inc(newton, 1)
                dve.wait_ge(newton, k + 3)
                dve.tensor_scalar(rtmp[:, :], rtmp[:, :], -0.5 * X_SCALE, 1.5 * X_SCALE,
                                  ALU.mult, ALU.add).then_inc(newton, 1)
                dve.wait_ge(newton, k + 4)
                dve.tensor_tensor(scale[:, :], rtmp[:, :], rinv[:, :], ALU.mult).then_inc(newton, 1)

            def prepare(u, r):
                dve.wait_ge(newton, NEWTON * (u + 1))
                dve.wait_ge(hi_ready, NS * u)
                dve.wait_ge(lo_ready, NS * u)
                k = PREP * u
                for m in range(PER):
                    dve.tensor_scalar(xn[:, ROWS * m:ROWS * m + ROWS, PAD:PAD + SIDE],
                                      image(r, m).rearrange("p (n w) -> p n w", w=SIDE),
                                      negmean[:, m:m + 1], scale[:, m:m + 1],
                                      ALU.add, ALU.mult).then_inc(prepared, 1)
                def less(o, a, b, need):
                    if need:
                        dve.wait_ge(prepared, k + need)
                    dve.tensor_tensor(o, a, b, ALU.subtract).then_inc(prepared, 1)
                dq = 4 * QS
                less(e[:, 1, 0, :, 0:QS], xn[:, :, 1:1 + dq:4], xn[:, :, 3:3 + dq:4], 2)
                less(e[:, 1, 1, :, 0:QS], xn[:, :, 5:2 + dq:4], xn[:, :, 3:dq:4], 0)
                half = 2 * QS + 1
                less(d[:, 0, :, 0:half], xn[:, :, 0:2 * half:2], xn[:, :, 1:1 + 2 * half:2], 0)
                less(e[:, 0, 0, :, 0:QS], d[:, 0, :, 0:2 * QS:2], d[:, 0, :, 1:1 + 2 * QS:2], 5)
                less(e[:, 0, 1, :, 0:QS], d[:, 0, :, 2:1 + 2 * QS:2], d[:, 0, :, 1:1 + 2 * QS:2], 0)
                less(d[:, 1, :, 0:half], xn[:, :, 2:2 * half + 1:2], xn[:, :, 1:2 * half:2], 0)
                less(e[:, 2, 0, :, 0:QS], d[:, 1, :, 0:2 * QS:2], d[:, 1, :, 1:1 + 2 * QS:2], 8)
                less(e[:, 2, 1, :, 0:QS], d[:, 1, :, 2:1 + 2 * QS:2], d[:, 1, :, 1:1 + 2 * QS:2], 0)

            def low(u, par, s):
                dve.wait_ge(hi_ready, NS * u + s + 1)
                dve.tensor_tensor(split(xlo, par, s), as_images(stream(s)), split(xhi, par, s),
                                  ALU.subtract).then_inc(lo_ready, 1)

            def pairs(u, h, s):
                dve.wait_ge(conv_done, NS * u + s + 1)
                if s == 3:
                    dve.wait_ge(conv_summed, u + 1)
                dve.wait_ge(middle_ready, 3 * u + s % 3 + 1)
                dve.scalar_tensor_tensor(pair[:, s - 3, :], banks[(NS * h + s) % BANKS][:, 0:N], scales[:, 1:2],
                                         middle[:, s % 3, :], ALU.mult, ALU.add).then_inc(pair_ready, 1)

            def step(u, h, streams, stats):
                if streams:
                    prepare(u + 1, (h + 1) % RING)
                    for s in range(NS):
                        low(u + 1, 1 - h % 2, s)
                if stats:
                    mean(u + 2)
                for s in range(3, 6):
                    pairs(u, h, s)
                if stats:
                    rstd(u + 2)
                for s in range(6, NS):
                    pairs(u, h, s)

            dve.wait_ge(weights_loaded, SETUP)
            dve.tensor_reduce(wmax[:, :], wts[:, :, :], AX.XY, ALU.max, apply_absolute_value=True
                              ).then_inc(wmax_ready, 1)
            dve.wait_ge(points_loaded, SETUP)
            dve.wait_ge(coloff_built, 2 * GROUPS)
            dve.tensor_scalar(pts[:, :, :], pts[:, :, :], -float(PAD), float(PAD), ALU.max, ALU.min).then_inc(hats, 1)
            dve.wait_ge(hats, 1)
            for r in range(TAPS):
                dve.tensor_scalar(hath[:, r, :], pts[:, 0, :], float(PAD), -float(TAPS - 1 - r),
                                  ALU.add, ALU.add).then_inc(hats, 1)
            for a in range(2):
                dve.tensor_scalar(hatw[:, a, :], pts[:, 1, :], float(PAD), coloff[:, a:a + 1],
                                  ALU.add, ALU.add).then_inc(hats, 1)
            k = 1 + TAPS + 2
            dve.wait_ge(hats, k)
            for t in (hath, hatw):
                dve.scalar_tensor_tensor(t[:, :, :], t[:, :, :], -1.0, t[:, :, :], ALU.mult, ALU.min).then_inc(hats, 1)
            dve.wait_ge(hats, k + 2)
            for t in (hath, hatw):
                dve.tensor_scalar(t[:, :, :], t[:, :, :], 1.0, 0.0, ALU.add, ALU.max).then_inc(hats, 1)
            dve.wait_ge(hats, k + 4)
            for a in range(2):
                dve.tensor_tensor(hat2[:, a, :, :], hath[:, :, :],
                                  hatw[:, a:a + 1, :].broadcast_to([128, TAPS, POINTS]), ALU.mult).then_inc(hats, 1)
            dve.wait_ge(hats, k + 6)
            flat = hat2[:, :, :, :].rearrange("p a r k -> p (a r) k")
            dve.tensor_tensor(prod, flat.unsqueeze(2).broadcast_to([128, 2 * TAPS, CH, POINTS]),
                              wts[:, :, :].unsqueeze(1).broadcast_to([128, 2 * TAPS, CH, POINTS]),
                              ALU.mult).then_inc(hats, 1)
            dve.wait_ge(hats, k + 7)
            dve.tensor_reduce(kern[:, :, :].rearrange("p a (r o) -> p (a r) o", o=CH), prod, AX.X, ALU.add
                              ).then_inc(kern_ready, 1)
            dve.wait_ge(wmax_row, 1)
            dve.tensor_reduce(srow[:, 0:1], mean_ps[0:1, 0:128], AX.X, ALU.max).then_inc(srow_step, 1)
            dve.wait_ge(srow_step, 1)
            dve.tensor_scalar(srow[:, 1:2], srow[:, 0:1], 2.0 ** -80, None, ALU.max).then_inc(srow_step, 1)
            dve.wait_ge(srow_step, 2)
            dve.tensor_scalar(srow[:, 0:1].bitcast(i32), srow[:, 1:2].bitcast(i32), 0x7F800000, None,
                              ALU.bitwise_and).then_inc(srow_step, 1)
            dve.wait_ge(srow_step, 3)
            dve.reciprocal(srow[:, 1:2], srow[:, 0:1]).then_inc(srow_step, 1)
            dve.wait_ge(srow_step, 4)
            dve.tensor_scalar(srow[:, 2:3], srow[:, 1:2], W_SCALE, None, ALU.mult).then_inc(srow_step, 1)
            dve.tensor_scalar(srow[:, 3:4], srow[:, 0:1], 1.0 / (W_SCALE * X_SCALE), None,
                              ALU.mult).then_inc(srow_step, 1)
            dve.wait_ge(scales_in_psum, 1)
            dve.tensor_copy(scales[:, :], var_ps[:, 0:2]).then_inc(scales_ready, 1)
            mean(0)
            rstd(0)
            dve.wait_ge(xn_zeroed, 1)
            prepare(0, 0)
            for s in range(NS):
                low(0, 0, s)
            mean(1)
            rstd(1)
            dve.wait_ge(kernel_spread, GROUPS * GROUPS * DMA)
            dve.tensor_tensor(filt[:, 1, :, :], filt[:, 0, :, :], filt[:, 2, :, :], ALU.add).then_inc(filt_summed, 1)
            dve.wait_ge(filt_summed, 1)
            for q in range(2):
                last = dve.tensor_tensor(filtsum[:, :, q, :], filt[:, :, 2 * q, :], filt[:, :, 2 * q + 1, :], ALU.add)
            last.then_inc(filt_summed, 1)
            dve.wait_ge(filt_summed, 2)
            for n, (i, j) in enumerate(STREAMS):
                dve.wait_ge(whi_ready, n + 1)
                dve.scalar_tensor_tensor(scaled(wlo, i, j), filter_of(i, j), scales[:, 0:1], scaled(whi, i, j),
                                         ALU.mult, ALU.subtract).then_inc(wlo_ready, 1)
            with dve.Fori(0, UNITS // RING - 1) as it:
                for h in range(RING):
                    step(it * RING + h, h, True, True)
            for h in range(RING):
                u = UNITS - RING + h
                step(u, h, u + 1 < UNITS, u + 2 < UNITS)

        @block.gpsimd
        def _(pool):
            for g in range(GROUPS):
                for a in range(2):
                    pool.memset(coloff[32 * g:32 * g + 32, a:a + 1], -2.0 * g - a).then_inc(coloff_built, 1)
            pool.wait_ge(coloff_built, 2 * GROUPS)
            pool.memset(filt[:, :, :, :], 0.0).then_inc(filt_zeroed, 1)
            pool.memset(fold[:, :], 0.0).then_inc(fold_built, 1)
            pool.memset(ident[:, :], 0.0).then_inc(ident_built, 1)
            pool.memset(ones[:, :], 1.0).then_inc(ones_built, 1)
            pool.wait_ge(ident_built, 1)
            pool.affine_select(out=ident[:, :], in_=ident[:, :], compare_op=ALU.not_equal, fill=1.0,
                               base=0, pattern=[[-1, 128]], channel_multiplier=1).then_inc(ident_built, 1)
            for n, k in enumerate(range(1 - GROUPS, GROUPS)):
                pool.wait_ge(fold_built, n + 1)
                pool.affine_select(out=fold[:, :], in_=fold[:, :], compare_op=ALU.not_equal,
                                   fill=-1.0 / (SIDE * SIDE), base=32 * k, pattern=[[-1, 128]],
                                   channel_multiplier=1).then_inc(fold_built, 1)
            pool.memset(xn[:, :, :], 0.0).then_inc(xn_zeroed, 1)
            pool.memset(xhi[:, :, :, :, :, :], 0.0).then_inc(pads_zeroed, 1)
            pool.memset(xlo[:, :, :, :, :, :], 0.0).then_inc(pads_zeroed, 1)

            def spread(g, q):
                pool.dma_start(filt[32 * g:32 * g + 32, 0:3:2, q, (g + 1) * CH:(g + 1 + TAPS) * CH],
                               kern[32 * q:32 * q + 32, :, :]).then_inc(kernel_spread, DMA)

            pool.wait_ge(filt_zeroed, 1)
            pool.wait_ge(kern_ready, 1)
            for g in range(GROUPS):
                for q in range(GROUPS):
                    spread(g, q)

            def step(u, h, before, first=False):
                cols = conv.rearrange("p (l q k) -> p l q k", q=QW, k=4)
                if h or not first:
                    pool.wait_ge(result_ready, u)
                for a in range(2):
                    for b in range(2):
                        pool.wait_ge(pair_ready, 6 * u + 6 + 3 * a + b + 2)
                        last = pool.tensor_tensor(
                            cols[:, :, :, 2 * b + a],
                            pair[:, 3 * a + b, :].rearrange("p (l q) -> p l q", q=QW),
                            pair[:, 3 * a + b + 1, :].rearrange("p (l q) -> p l q", q=QW), ALU.add)
                last.then_inc(conv_summed, 1)
                pool.wait_ge(conv_summed, u + 2)
                if h >= 2 or not first:
                    pool.wait_ge(stored[h % 2], LOAD * before)
                pool.tensor_tensor(result[:, h % 2, :].rearrange("p (m n) -> p m n", m=PER),
                                   conv.rearrange("p (m n) -> p m n", m=PER), xraw[:, PER * h:PER * (h + 1), :],
                                   ALU.add).then_inc(result_ready, 1)

            pool.memset(conv[:, PER * PLANE - 1:PER * PLANE], 0.0).then_inc(pair_ready, 6)
            pool.memset(conv[:, PER * PLANE - 2:PER * PLANE - 1], 0.0).then_inc(conv_summed, 1)
            for h in range(RING):
                step(h, h, h // 2, True)
            with pool.Fori(1, UNITS // RING) as it:
                for h in range(RING):
                    step(it * RING + h, h, it * (RING // 2) + h // 2)

        @block.tensor
        def _(pe):
            pe.wait_ge(wmax_ready, 1)
            pe.wait_ge(ident_built, 2)
            pe.matmul(mean_ps[0:1, 0:128], wmax[:, :], ident[:, :], start=True, stop=True).then_inc(wmax_row, 1)
            pe.wait_ge(srow_step, 6)
            pe.wait_ge(ones_built, 1)
            pe.matmul(var_ps[:, 0:2], ones[:, :], srow[:, 2:4], start=True, stop=True).then_inc(scales_in_psum, 1)
            pe.wait_ge(fold_built, 2 * GROUPS)
            pe.wait_ge(scales_ready, 1)

            def mean(u):
                pe.wait_ge(sum_ready, u + 1)
                pe.wait_ge(negmean_ready, u)
                pe.matmul(mean_ps[:, 0:PER], fold[:, :], xsum[:, :], start=True, stop=True).then_inc(mean_in_psum, 1)

            def variance(u):
                pe.wait_ge(ssq_ready, u + 1)
                pe.wait_ge(var_ready, u)
                pe.matmul(var_ps[:, 0:PER], fold[:, :], ssq[:, :], start=True, stop=True).then_inc(var_in_psum, 1)

            def convolve(u, h, s, first):
                i, j = STREAMS[s]
                taps = 1 if (i, j) == (2, 2) else 2
                if first:
                    pe.wait_ge(wlo_ready, s + 1)
                pe.wait_ge(lo_ready, NS * u + s + 1)
                if s < BANKS:
                    pe.wait_ge(pair_ready, 6 * u + s + 1)
                else:
                    pe.wait_ge(middle_ready, 3 * u + s - BANKS + 1)
                into = banks[(NS * h + s) % BANKS][:, 0:N].rearrange("p (m n q) -> p m n q", m=PER, q=QW)
                for q in range(taps):
                    for t in range(3):
                        v = (2 - t) * GROUPS * CH
                        for n, (w, xs) in enumerate(((whi, xhi), (whi, xlo), (wlo, xhi))):
                            last = pe.matmul(into, w[:, i, j, q, v:v + 128],
                                             xs[:, h, s, :, t:t + ROWS, q:q + QW],
                                             start=q == t == n == 0, stop=q == taps - 1 and t == n == 2)
                last.then_inc(conv_done, 1)

            def step(u, h, stats, first=False):
                for s in range(NS):
                    if stats and s == 3:
                        mean(u + 2)
                    if stats and s == 6:
                        variance(u + 2)
                    convolve(u, h, s, first)

            for u in range(2):
                mean(u)
                variance(u)
            pe.wait_ge(wlo_ready, NS)
            with pe.Fori(0, UNITS // 2 - 1) as it:
                for h in range(2):
                    step(it * 2 + h, h, True)
            step(UNITS - 2, 0, False)
            step(UNITS - 1, 1, False)


def kernel(**inputs):
    import numpy as np
    import concourse.bacc as bacc
    from concourse.bass_utils import run_bass_kernel_spmd

    nc = bacc.Bacc("TRN2", target_bir_lowering=False, num_devices=1)
    arrays, args = {}, []
    for name in ("x", "L0_conv_weight", "L0_conv_P", "L0_conv_bias"):
        a = np.ascontiguousarray(inputs[name])
        arrays[name] = a
        args.append(nc.dram_tensor(name, a.shape, mybir.dt.from_np(a.dtype), kind="ExternalInput").ap())
    args.append(nc.dram_tensor("out", (BATCH, CH, SIDE, SIDE), mybir.dt.float32, kind="ExternalOutput").ap())
    build(nc, *args)
    r = run_bass_kernel_spmd(nc, [arrays], core_ids=[0])
    return r.results[0]["out"]
```

```python
import concourse.bass as bass
from concourse import mybir
from contextlib import ExitStack

BATCH, CH, SIDE = 32, 32, 56
TAPS = 7
POINTS = 9
GROUPS = 4
ROWS = SIDE // GROUPS
PER = 2
UNITS = BATCH // PER
LINES = PER * ROWS
PLANE = ROWS * SIDE
PAD = TAPS // 2
WPAD = 64
QW = SIDE // 4
QS = QW + 1
QP = 16
N = LINES * QW
SLOTS = ROWS + 1
XLINES = PER * SLOTS
BELOW = ROWS - 1
V = 12
HALF = 64
VO = V * CH
X_SCALE = 256.0
W_SCALE = 2048.0
EPS = 1e-5
RING = 4
BANKS = 6
STREAMS = [(1, 0), (1, 1), (1, 2), (0, 0), (0, 1), (0, 2), (2, 0), (2, 1), (2, 2)]
NS = len(STREAMS)
PACKED = NS - 1
BY_DVE = 3
PARTS = 4
STEP_OF = [5, 4, 6, 8, 7, 9, 11, 10, 12]
PREP = 12
NEWTON = 5
DMA = 16
LOAD = PER * GROUPS * DMA


def build(nc, x, weight, P, bias, out):
    fp32 = mybir.dt.float32
    fp16 = mybir.dt.float16
    i32 = mybir.dt.int32
    ALU = mybir.AluOpType
    ACT = mybir.ActivationFunctionType
    AX = mybir.AxisListType

    ctx = ExitStack()
    with ctx:
        def sb(name, shape, dt):
            return ctx.enter_context(nc.sbuf_tensor(name, shape, dt))

        def sem(name):
            return ctx.enter_context(nc.semaphore(name))

        xraw = sb("xraw", [128, RING * PER, PLANE], fp32)
        junk = sb("junk", [128, 2, PER, PLANE], fp16)
        xn = sb("xn", [128, XLINES, WPAD], fp32)
        d = sb("d", [128, 2, XLINES, WPAD // 2], fp32)
        e = sb("e", [128, 3, 2, XLINES, QP], fp32)
        xhi = sb("xhi", [128, 2, NS, PER, SLOTS, QP], fp16)
        xlo = sb("xlo", [128, 2, NS, PER, SLOTS, QP], fp16)
        packed = sb("packed", [128, 2, 2, PACKED, PER, BELOW, QP], fp16)
        late = sb("late", [128, 9 * N + PER * PLANE], fp32)
        middle = late[:, 0:3 * N].rearrange("p (j n) -> p j n", j=3)
        pair = late[:, 3 * N:9 * N].rearrange("p (j n) -> p j n", j=6)
        part = late[:, 9 * N:9 * N + 4 * N].rearrange("p (k n) -> p k n", k=4)
        prod = late[:, 0:2 * TAPS * CH * POINTS].rearrange("p (a o k) -> p a o k", o=CH, k=POINTS)
        result = sb("result", [128, 2, PER * PLANE], fp32)
        fold = sb("fold", [128, 128], fp32)
        xsum = sb("xsum", [128, PER], fp32)
        negmean = sb("negmean", [128, PER], fp32)
        ssq = sb("ssq", [128, PER], fp32)
        var = sb("var", [128, PER], fp32)
        std = sb("std", [128, PER], fp32)
        rinv = sb("rinv", [128, PER], fp32)
        rtmp = sb("rtmp", [128, PER], fp32)
        scale = sb("scale", [128, PER], fp32)
        ident = sb("ident", [128, 128], fp32)
        ones = sb("ones", [1, 128], fp32)
        pts = sb("pts", [128, 2, POINTS], fp32)
        setup0 = packed[:, 0, :, :, :, :, :].rearrange("p a s m n q -> p (a s m n q)").bitcast(fp32)
        setup1 = packed[:, 1, :, :, :, :, :].rearrange("p a s m n q -> p (a s m n q)").bitcast(fp32)
        wnat = setup0[0:CH, 0:GROUPS * CH * POINTS].rearrange("p (g w) -> p g w", g=GROUPS)
        coloff = sb("coloff", [128, 2], fp32)
        wts = sb("wts", [128, POINTS, CH], fp32)
        hath = sb("hath", [128, TAPS, POINTS], fp32)
        hatw = sb("hatw", [128, 2, POINTS], fp32)
        hat2 = sb("hat2", [128, 2, TAPS, POINTS], fp32)
        kern = sb("kern", [128, 2, TAPS * CH], fp32)
        raw = result[:, :, :].rearrange("p a n -> p (a n)")[:, 0:8 * VO].rearrange("p (i q v) -> p i q v", i=2, q=4)
        outer = setup1[:, 0:8 * VO].rearrange("p (i q v) -> p i q v", i=2, q=4)
        inner = sb("inner", [128, 4, VO], fp32)
        filtsum = [late[:, a:a + 2 * VO].rearrange("p (q v) -> p q v", q=2) for a in (9 * N, 3 * N, 9 * N + 2 * VO)]
        whi = sb("whi", [128, 3, 3, 2, VO], fp16)
        wlo = sb("wlo", [128, 3, 3, 2, VO], fp16)
        whi_packed = sb("whi_packed", [128, 3, 3, 4 * CH], fp16)
        wlo_packed = sb("wlo_packed", [128, 3, 3, 4 * CH], fp16)
        wmax = sb("wmax", [CH, 1], fp32)
        srow = sb("srow", [1, 4], fp32)
        unused = sb("unused", [1, 1], fp32)
        credit = sb("credit", [1, 2], fp32)
        scales = sb("scales", [128, 2], fp32)
        biascol = sb("biascol", [128, 1], fp32)

        banks = [ctx.enter_context(nc.psum_tensor(f"bank{k}", [128, 512], fp32)) for k in range(BANKS)]
        mean_ps = ctx.enter_context(nc.psum_tensor("mean_ps", [128, 512], fp32))
        var_ps = ctx.enter_context(nc.psum_tensor("var_ps", [128, 512], fp32))

        x_loaded = [sem("x_loaded_even"), sem("x_loaded_odd")]
        stored = [sem("stored_even"), sem("stored_odd")]
        points_loaded = sem("points_loaded")
        weights_loaded = sem("weights_loaded")
        weights_turned = sem("weights_turned")
        weights_copied = sem("weights_copied")
        bias_loaded = sem("bias_loaded")
        spread_by_sync = sem("spread_by_sync")
        spread_by_pool = sem("spread_by_pool")
        sum_ready = sem("sum_ready")
        mean_in_psum = sem("mean_in_psum")
        negmean_ready = sem("negmean_ready")
        ssq_ready = sem("ssq_ready")
        var_in_psum = sem("var_in_psum")
        var_ready = sem("var_ready")
        std_ready = sem("std_ready")
        newton = sem("newton")
        prepared = sem("prepared")
        hi_ready = sem("hi_ready")
        lo_ready = sem("lo_ready")
        packed_by_act = sem("packed_by_act")
        packed_by_dve = sem("packed_by_dve")
        conv_done = sem("conv_done")
        middle_ready = sem("middle_ready")
        pair_ready = sem("pair_ready")
        image_added = sem("image_added")
        last_image_added = sem("last_image_added")
        final_added = sem("final_added")
        fold_built = sem("fold_built")
        ident_built = sem("ident_built")
        ones_built = sem("ones_built")
        coloff_built = sem("coloff_built")
        filt_zeroed = sem("filt_zeroed")
        xn_zeroed = sem("xn_zeroed")
        hats = sem("hats")
        wmax_ready = sem("wmax_ready")
        wmax_row = sem("wmax_row")
        srow_step = sem("srow_step")
        scales_in_psum = sem("scales_in_psum")
        scales_ready = sem("scales_ready")
        kern_ready = sem("kern_ready")
        filt_summed = sem("filt_summed")
        whi_ready = sem("whi_ready")
        wlo_by_dve = sem("wlo_by_dve")
        wlo_by_pool = sem("wlo_by_pool")
        filt_summed_by_pool = sem("filt_summed_by_pool")
        products_by_pool = sem("products_by_pool")
        turned_by_pool = sem("turned_by_pool")
        whi_packs = sem("whi_packs")
        wlo_packs = sem("wlo_packs")
        edges_zeroed = sem("edges_zeroed")

        block = ctx.enter_context(nc.Block())

        def image(r, m):
            return xraw[:, r * PER + m, :]

        def dram_rows(t, u, m, g):
            return t[bass.ds(u * PER + m, 1), :, (g + 1) % GROUPS::GROUPS, :].rearrange("m c n w -> (m c) n w")

        def stream(s):
            i, j = STREAMS[s]
            if j != 1:
                return e[:, i, j // 2, :, 0:width(s)]
            if i == 1:
                return xn[:, :, 3:4 * width(s):4]
            return d[:, i // 2, :, 1:2 * width(s):2]

        def width(s):
            return QS - 1 if STREAMS[s] in ((1, 1), (1, 2), (2, 1), (2, 2)) else QS

        def split(t, par, s):
            return t[:, par, s, :, :, 0:width(s)]

        def as_images(ap):
            return ap.rearrange("p (m n) w -> p m n w", m=PER)

        def filter_of(i, j):
            return filtsum[i] if j == 1 else level_one(i, j // 2)

        def level_one(i, m):
            return inner[:, m::2, :] if i == 1 else outer[:, i // 2, m::2, :]

        TURNS = [((1, 4), (0, 3)), ((0, 1), (3, 4))]

        def phases(ap, a, b):
            return ap.rearrange("p q (r v) -> p q r v", v=GROUPS * CH)[:, :, :, a * CH:b * CH]

        def turn(eng, i):
            for (a, b), (c, f) in TURNS:
                last = eng.tensor_copy(phases(outer[:, i // 2, :, :], c, f), phases(raw[:, i // 2, :, :], a, b))
            return last

        def pack_images(op, half, par, which, s0, s1):
            src = (xhi, xlo)[which]
            return op(packed[HALF * half:HALF * (half + 1), par, which, s0:s1, :, :, 0:QW].rearrange(
                          "p s m n q -> p (s m) n q"),
                      src[0:HALF, par, s0:s1, :, 2:SLOTS, half:half + QW].rearrange("p s m n q -> p (s m) n q"))

        def pack_filter(op, dst, src, i):
            for half in range(2):
                last = op(dst[HALF * half:HALF * (half + 1), i, :, :], src[0:HALF, i, :, half, 0:GROUPS * CH])
            return last

        def spread(queue, pieces, done):
            queue.wait_ge(filt_zeroed, 2)
            queue.wait_ge(kern_ready, 1)
            for g, q in pieces:
                queue.dma_start(raw[32 * g:32 * g + 32, :, q, (g + 2) * CH:(g + 2 + TAPS) * CH],
                                kern[32 * q:32 * q + 32, :, :]).then_inc(done, DMA)

        pieces = [(g, q) for g in range(GROUPS) for q in range(GROUPS)]
        by_pool = 6

        def cols(t, k):
            return t.rearrange("p (l q k) -> p l q k", q=QW, k=4)[:, :, :, k]

        def lines(ap):
            return ap.rearrange("p (l q) -> p l q", q=QW)

        def add_image(eng, h, k):
            photo = xraw[:, PER * h:PER * (h + 1), :].rearrange("p m n -> p (m n)")
            return eng.tensor_tensor(lines(part[:, k, :]), lines(pair[:, 3 * (k // 2) + k % 2, :]),
                                     cols(photo, 2 * (k % 2) + k // 2), ALU.add)

        def add_pair(eng, h, k):
            return eng.tensor_tensor(cols(result[:, h % 2, :], 2 * (k % 2) + k // 2), lines(part[:, k, :]),
                                     lines(pair[:, 3 * (k // 2) + k % 2 + 1, :]), ALU.add)

        def products(eng, a):
            return eng.tensor_tensor(prod[:, TAPS * a:TAPS * (a + 1), :, :],
                                     hat2[:, a, :, :].unsqueeze(2).broadcast_to([128, TAPS, CH, POINTS]),
                                     wts[:, :, :].rearrange("p k o -> p o k").unsqueeze(1).broadcast_to(
                                         [128, TAPS, CH, POINTS]), ALU.mult)

        def sum_filters(eng, i):
            return eng.tensor_tensor(filtsum[i], level_one(i, 0), level_one(i, 1), ALU.add)

        def low_filter(eng, n):
            i, j = STREAMS[n]
            eng.wait_ge(whi_ready, n + 1)
            return eng.tensor_tensor(wlo[:, i, j, :, :], filter_of(i, j), whi[:, i, j, :, :], ALU.subtract)

        @block.sync
        def _(sp):
            def load(u, r):
                for m in range(PER):
                    for g in range(GROUPS):
                        sp.dma_start(image(r, m)[32 * g:32 * g + 32, :].rearrange("c (n w) -> c n w", w=SIDE),
                                     dram_rows(x, u, m, g)).then_inc(x_loaded[r % 2], DMA)

            def finished(u):
                sp.wait_ge(final_added, PARTS * u + 2 * PARTS)

            def store(u, par):
                for m in range(PER):
                    for g in range(GROUPS):
                        sp.dma_start(dram_rows(out, u, m, g),
                                     result[32 * g:32 * g + 32, par, PLANE * m:PLANE * (m + 1)].rearrange(
                                         "c (n w) -> c n w", w=SIDE)).then_inc(stored[par], DMA)

            sp.dma_start(wnat[:, :, :], weight.rearrange("o (a c) k -> o a (c k)", a=1)
                          .broadcast_to([CH, GROUPS, CH * POINTS])).then_inc(weights_loaded, DMA)
            for t in range(2):
                sp.dma_start(pts[:, t, :], P[t:t + 1, :, :].broadcast_to([GROUPS, CH, POINTS])
                              ).then_inc(points_loaded, DMA)
            load(0, 0)
            load(1, 1)
            sp.dma_start(biascol[:, :], bias.rearrange("(a c b) -> a c b", a=1, b=1)
                          .broadcast_to([GROUPS, CH, 1])).then_inc(bias_loaded, DMA)
            spread(sp, pieces[by_pool:], spread_by_sync)
            sp.wait_ge(sum_ready, 1)
            load(2, 2)
            sp.wait_ge(sum_ready, 2)
            load(3, 3)
            with sp.Fori(0, UNITS // RING - 1) as it:
                for h in range(RING):
                    u = it * RING + h
                    finished(u)
                    store(u, h % 2)
                    sp.wait_ge(sum_ready, u + 3)
                    load(u + RING, h)
            for u in range(UNITS - RING, UNITS):
                finished(u)
                store(u, u % 2)
            for par in range(2):
                sp.wait_ge(stored[par], LOAD * (UNITS // 2))

        @block.scalar
        def _(act):
            act.wait_ge(ones_built, 1)
            act.activation(unused[:, :], ones[:, 0:1], ACT.Sqrt)

            def sums(u, r, nth):
                act.wait_ge(x_loaded[r % 2], LOAD * (nth + 1))
                act.wait_ge(mean_in_psum, u)
                for m in range(PER):
                    last = act.activation(junk[:, r % 2, m, :], image(r, m), ACT.Identity, accum_out=xsum[:, m:m + 1])
                last.then_inc(sum_ready, 1)

            def squares(u, r):
                act.wait_ge(negmean_ready, u + 1)
                for m in range(PER):
                    last = act.activation(junk[:, r % 2, m, :], image(r, m), ACT.Square, bias=negmean[:, m:m + 1],
                                          accum_out=ssq[:, m:m + 1])
                last.then_inc(ssq_ready, 1)

            def root(u):
                act.wait_ge(var_ready, u + 1)
                act.activation(std[:, :], var[:, :], ACT.Sqrt).then_inc(std_ready, 1)

            def high(u, par, s):
                act.wait_ge(prepared, PREP * u + STEP_OF[s])
                act.activation(split(xhi, par, s), as_images(stream(s)), ACT.Copy).then_inc(hi_ready, 1)

            def copy(o, i):
                return act.activation(o, i, ACT.Copy)

            def pack(u, par, s0, s1):
                act.wait_ge(packed_by_dve, PACKED * u + s1)
                pack_images(copy, 1, par, 0, s0, s1)
                pack_images(copy, 1, par, 1, s0, s1).then_inc(packed_by_act, s1 - s0)

            def step(u, h, nth, streams, stats, early):
                def mid(j):
                    act.wait_ge(conv_done, NS * u + j + 1)
                    act.wait_ge(pair_ready, 6 * u + 4 + j)
                    act.activation(middle[:, j, :], banks[(NS * h + j) % BANKS][:, 0:N], ACT.Identity,
                                   bias=biascol[:, 0:1] if j == 1 else 0.0,
                                   scale=scales[:, 1:2]).then_inc(middle_ready, 1)
                for j in range(3):
                    mid(j)
                    if streams:
                        for s in range(3 * j, 3 * j + 3):
                            high(u + 1, 1 - h % 2, s)
                if stats:
                    squares(u + 2, (h + 2) % RING)
                if streams:
                    pack(u + 1, 1 - h % 2, 0, PACKED)
                if stats:
                    root(u + 2)
                if early:
                    sums(u + 3, (h + 3) % RING, nth)

            act.wait_ge(weights_turned, 1)
            act.activation(wts[:, :, :], banks[0][:, 0:POINTS * CH].rearrange("p (k o) -> p k o", o=CH), ACT.Copy
                           ).then_inc(weights_copied, 1)
            sums(0, 0, 0)
            squares(0, 0)
            root(0)
            sums(1, 1, 0)
            for s in range(NS):
                high(0, 0, s)
                if s == 3:
                    squares(1, 1)
            for n, (i, j) in enumerate(STREAMS):
                if n == 4:
                    root(1)
                    sums(2, 2, 1)
                if i == 1:
                    act.wait_ge(filt_summed, {0: 1, 2: 2, 1: 3}[j])
                elif j == 1:
                    act.wait_ge(filt_summed_by_pool, {0: 1, 2: 2}[i])
                else:
                    act.wait_ge(turned_by_pool, {0: 1, 2: 2}[i])
                copy(whi[:, i, j, :, :], filter_of(i, j)).then_inc(whi_ready, 1)
                if n % 3 == 2:
                    act.wait_ge(whi_ready, n + 1)
                    pack_filter(copy, whi_packed, whi, i).then_inc(whi_packs, 1)
                    pack(0, 0, n - 2, min(n + 1, PACKED))
            act.wait_ge(bias_loaded, DMA)
            with act.Fori(0, UNITS // RING - 1) as it:
                for h in range(RING):
                    step(it * RING + h, h, it * (RING // 2) + (h + 3) // 2, True, True, True)
            for h in range(RING):
                u = UNITS - RING + h
                step(u, h, (u + 3) // 2, u + 1 < UNITS, u + 2 < UNITS, u + 3 < UNITS)

        @block.vector
        def _(dve):
            def mean(u):
                dve.wait_ge(mean_in_psum, u + 1)
                dve.tensor_copy(negmean[:, :], mean_ps[:, 0:PER]).then_inc(negmean_ready, 1)

            def rstd(u):
                dve.wait_ge(var_in_psum, u + 1)
                dve.tensor_scalar(var[:, :], var_ps[:, 0:PER], -1.0, EPS, ALU.mult, ALU.add).then_inc(var_ready, 1)
                dve.wait_ge(std_ready, u + 1)
                k = NEWTON * u
                dve.reciprocal(rinv[:, :], std[:, :]).then_inc(newton, 1)
                dve.wait_ge(newton, k + 1)
                dve.tensor_tensor(rtmp[:, :], rinv[:, :], rinv[:, :], ALU.mult).then_inc(newton, 1)
                dve.wait_ge(newton, k + 2)
                dve.tensor_tensor(rtmp[:, :], rtmp[:, :], var[:, :], ALU.mult).then_inc(newton, 1)
                dve.wait_ge(newton, k + 3)
                dve.tensor_scalar(rtmp[:, :], rtmp[:, :], -0.5 * X_SCALE, 1.5 * X_SCALE,
                                  ALU.mult, ALU.add).then_inc(newton, 1)
                dve.wait_ge(newton, k + 4)
                dve.tensor_tensor(scale[:, :], rtmp[:, :], rinv[:, :], ALU.mult).then_inc(newton, 1)

            def normalise(u, r):
                dve.wait_ge(newton, NEWTON * (u + 1))
                if not isinstance(u, int) or u > 0:
                    dve.wait_ge(hi_ready, NS * u)
                    dve.wait_ge(lo_ready, NS * u)
                for m in range(PER):
                    for a, b, slot in ((0, 96, 1), (96, 128, 0)):
                        line = SLOTS * m + slot
                        dve.tensor_scalar(xn[a:b, line:line + ROWS, PAD:PAD + SIDE],
                                          image(r, m)[a:b, :].rearrange("p (n w) -> p n w", w=SIDE),
                                          negmean[a:b, m:m + 1], scale[a:b, m:m + 1],
                                          ALU.add, ALU.mult).then_inc(prepared, 1)

            def differences(u, steps):
                def less(step, o, a, b, need):
                    if step in steps:
                        if need:
                            dve.wait_ge(prepared, PREP * u + need)
                        dve.tensor_tensor(o, a, b, ALU.subtract).then_inc(prepared, 1)
                half = 2 * QS + 1
                d0, d1 = d[:, 0, :, :], d[:, 1, :, :]
                less(5, e[:, 1, 0, :, 0:QS], xn[:, :, 1:4 * QS + 1:4], xn[:, :, 3:4 * QS:4], 4)
                less(6, e[:, 1, 1, :, 0:QS], xn[:, :, 5:4 * QS + 2:4], xn[:, :, 3:4 * QS:4], 0)
                less(7, d0[:, :, 0:half], xn[:, :, 0:2 * half:2], xn[:, :, 1:2 * half:2], 0)
                less(8, e[:, 0, 0, :, 0:QS], d0[:, :, 0:2 * QS:2], d0[:, :, 1:2 * QS:2], 7)
                less(9, e[:, 0, 1, :, 0:QS], d0[:, :, 2:2 * QS + 1:2], d0[:, :, 1:2 * QS:2], 0)
                less(10, d1[:, :, 0:half], xn[:, :, 2:2 * half + 1:2], xn[:, :, 1:2 * half:2], 0)
                less(11, e[:, 2, 0, :, 0:QS], d1[:, :, 0:2 * QS:2], d1[:, :, 1:2 * QS:2], 10)
                less(12, e[:, 2, 1, :, 0:QS], d1[:, :, 2:2 * QS + 1:2], d1[:, :, 1:2 * QS:2], 0)

            def low(u, par, s):
                dve.wait_ge(hi_ready, NS * u + s + 1)
                dve.tensor_tensor(split(xlo, par, s), as_images(stream(s)), split(xhi, par, s),
                                  ALU.subtract).then_inc(lo_ready, 1)

            def pairs(u, h, s):
                dve.wait_ge(conv_done, NS * u + s + 1)
                if s == 3:
                    dve.wait_ge(final_added, PARTS * u + PARTS)
                dve.wait_ge(middle_ready, 3 * u + s % 3 + 1)
                dve.scalar_tensor_tensor(pair[:, s - 3, :], banks[(NS * h + s) % BANKS][:, 0:N], scales[:, 1:2],
                                         middle[:, s % 3, :], ALU.mult, ALU.add).then_inc(pair_ready, 1)

            def pack(u, par, s0, s1):
                dve.wait_ge(lo_ready, NS * u + s1)
                pack_images(dve.tensor_copy, 0, par, 0, s0, s1)
                pack_images(dve.tensor_copy, 0, par, 1, s0, s1).then_inc(packed_by_dve, s1 - s0)

            def step(u, h, streams, stats):
                if streams:
                    normalise(u + 1, (h + 1) % RING)
                    differences(u + 1, range(5, PREP + 1))
                if stats:
                    mean(u + 2)
                if streams:
                    for s in range(NS):
                        low(u + 1, 1 - h % 2, s)
                    if isinstance(u, int) and u == 0:
                        dve.wait_ge(wlo_by_pool, NS - BY_DVE)
                        pack_filter(dve.tensor_copy, wlo_packed, wlo, 2).then_inc(wlo_packs, 1)
                    pack(u + 1, 1 - h % 2, 0, PACKED)
                for s in range(3, 7):
                    pairs(u, h, s)
                if stats:
                    rstd(u + 2)
                for s in range(7, NS):
                    pairs(u, h, s)

            for g in range(GROUPS):
                for a in range(2):
                    dve.memset(coloff[32 * g:32 * g + 32, a:a + 1], -2.0 * g - a).then_inc(coloff_built, 1)
            dve.memset(ones[:, :], 1.0).then_inc(ones_built, 1)
            dve.memset(xn[:, :, 0:PAD], 0.0).then_inc(xn_zeroed, 1)
            dve.memset(xn[:, :, PAD + SIDE:WPAD], 0.0).then_inc(xn_zeroed, 1)
            dve.memset(xn[:, ::SLOTS, PAD:PAD + SIDE], 0.0).then_inc(xn_zeroed, 1)
            dve.memset(xn[96:128, ROWS::SLOTS, PAD:PAD + SIDE], 0.0).then_inc(xn_zeroed, 1)
            dve.memset(raw[:, 0, :, :], 0.0).then_inc(filt_zeroed, 1)
            dve.wait_ge(weights_loaded, DMA)
            dve.tensor_reduce(wmax[:, :], wnat[:, 0, :], AX.X, ALU.max, apply_absolute_value=True
                              ).then_inc(wmax_ready, 1)
            dve.wait_ge(points_loaded, 2 * DMA)
            dve.tensor_scalar(pts[:, :, :], pts[:, :, :], -float(PAD), float(PAD), ALU.max, ALU.min).then_inc(hats, 1)
            dve.wait_ge(hats, 1)
            dve.wait_ge(coloff_built, 2 * GROUPS)
            for r in range(TAPS):
                dve.tensor_scalar(hath[:, r, :], pts[:, 0, :], float(PAD), -float(TAPS - 1 - r),
                                  ALU.add, ALU.add).then_inc(hats, 1)
            for a in range(2):
                dve.tensor_scalar(hatw[:, a, :], pts[:, 1, :], float(PAD), coloff[:, a:a + 1],
                                  ALU.add, ALU.add).then_inc(hats, 1)
            k = 1 + TAPS + 2
            dve.wait_ge(hats, k)
            for t in (hath, hatw):
                dve.scalar_tensor_tensor(t[:, :, :], t[:, :, :], -1.0, t[:, :, :], ALU.mult, ALU.min).then_inc(hats, 1)
            dve.wait_ge(hats, k + 2)
            for t in (hath, hatw):
                dve.tensor_scalar(t[:, :, :], t[:, :, :], 1.0, 0.0, ALU.add, ALU.max).then_inc(hats, 1)
            dve.wait_ge(hats, k + 4)
            for a in range(2):
                dve.tensor_tensor(hat2[:, a, :, :], hath[:, :, :],
                                  hatw[:, a:a + 1, :].broadcast_to([128, TAPS, POINTS]), ALU.mult).then_inc(hats, 1)
            for t in (xhi, xlo):
                dve.memset(t[:, :, 0:PACKED, :, :, QS - 1:QS].rearrange("p a s m n q -> p a (s m n) q"),
                           0.0).then_inc(edges_zeroed, 1)
            dve.wait_ge(hats, k + 6)
            dve.wait_ge(weights_copied, 1)
            products(dve, 0).then_inc(hats, 1)
            dve.wait_ge(wmax_row, 1)
            dve.tensor_reduce(srow[:, 0:1], banks[1][0:1, 0:CH], AX.X, ALU.max).then_inc(srow_step, 1)
            dve.wait_ge(srow_step, 1)
            dve.tensor_scalar(srow[:, 1:2], srow[:, 0:1], 2.0 ** -80, None, ALU.max).then_inc(srow_step, 1)
            dve.wait_ge(srow_step, 2)
            dve.tensor_scalar(srow[:, 0:1].bitcast(i32), srow[:, 1:2].bitcast(i32), 0x7F800000, None,
                              ALU.bitwise_and).then_inc(srow_step, 1)
            dve.wait_ge(srow_step, 3)
            dve.reciprocal(srow[:, 1:2], srow[:, 0:1]).then_inc(srow_step, 1)
            dve.wait_ge(srow_step, 4)
            dve.tensor_scalar(srow[:, 2:3], srow[:, 1:2], W_SCALE, None, ALU.mult).then_inc(srow_step, 1)
            dve.tensor_scalar(srow[:, 3:4], srow[:, 0:1], 1.0 / (W_SCALE * X_SCALE), None,
                              ALU.mult).then_inc(srow_step, 1)
            dve.wait_ge(hats, k + 7)
            for a in range(2):
                if a:
                    mean(0)
                    dve.wait_ge(products_by_pool, 1)
                dve.tensor_reduce(kern[:, a, :].rearrange("p (r o) -> p r o", o=CH),
                                  prod[:, TAPS * a:TAPS * (a + 1), :, :], AX.X, ALU.add).then_inc(hats, 1)
            dve.wait_ge(scales_in_psum, 1)
            dve.tensor_copy(scales[:, :], banks[2][:, 0:2]).then_inc(scales_ready, 1)
            dve.wait_ge(scales_ready, 1)
            dve.wait_ge(hats, k + 9)
            dve.tensor_scalar(kern[:, :, :], kern[:, :, :], scales[:, 0:1], None, ALU.mult).then_inc(kern_ready, 1)
            rstd(0)
            dve.wait_ge(xn_zeroed, 4)
            normalise(0, 0)
            differences(0, (5, 6))
            mean(1)
            differences(0, range(7, PREP + 1))
            dve.wait_ge(spread_by_sync, (GROUPS * GROUPS - by_pool) * DMA)
            dve.wait_ge(spread_by_pool, by_pool * DMA)
            dve.wait_ge(edges_zeroed, 2)
            for m in range(2):
                for (p, q), (c, f) in TURNS:
                    last = dve.tensor_tensor(phases(inner[:, m::2, :], c, f), phases(raw[:, 0, m::2, :], p, q),
                                             phases(raw[:, 1, m::2, :], p, q), ALU.add)
                last.then_inc(filt_summed, 1)
                if m == 0:
                    low(0, 0, 0)
            low_filter(dve, 0).then_inc(wlo_by_dve, 1)
            dve.wait_ge(filt_summed, 2)
            sum_filters(dve, 1).then_inc(filt_summed, 1)
            for n in range(1, NS):
                low(0, 0, n)
                if n < BY_DVE:
                    low_filter(dve, n).then_inc(wlo_by_dve, 1)
                if n == BY_DVE - 1:
                    pack(0, 0, 0, 3)
                    dve.wait_ge(wlo_by_dve, BY_DVE)
                    pack_filter(dve.tensor_copy, wlo_packed, wlo, 1).then_inc(wlo_packs, 1)
                if n == 5:
                    rstd(1)
                    pack(0, 0, 3, 6)
            pack(0, 0, 6, PACKED)
            dve.wait_ge(wlo_by_pool, 3)
            pack_filter(dve.tensor_copy, wlo_packed, wlo, 0).then_inc(wlo_packs, 1)
            for h in range(RING):
                step(h, h, True, True)
            with dve.Fori(1, UNITS // RING - 1) as it:
                for h in range(RING):
                    step(it * RING + h, h, True, True)
            for h in range(RING):
                u = UNITS - RING + h
                step(u, h, u + 1 < UNITS, u + 2 < UNITS)
            k = PARTS - 1
            dve.wait_ge(pair_ready, 6 * UNITS + 5)
            dve.wait_ge(final_added, PARTS * (UNITS - 1) + PARTS)
            add_image(dve, RING - 1, k).then_inc(last_image_added, 1)
            dve.wait_ge(pair_ready, 6 * UNITS + 6)
            dve.wait_ge(stored[1], LOAD * (UNITS // 2 - 1))
            dve.wait_ge(final_added, PARTS * UNITS + k)
            dve.wait_ge(last_image_added, 1)
            add_pair(dve, RING - 1, k).then_inc(final_added, 1)

        @block.gpsimd
        def _(pool):
            pool.memset(ident[:, :], 0.0).then_inc(ident_built, 1)
            pool.memset(fold[:, :], 0.0).then_inc(fold_built, 1)
            pool.wait_ge(ident_built, 1)
            pool.affine_select(out=ident[:, :], in_=ident[:, :], compare_op=ALU.not_equal, fill=1.0,
                               base=0, pattern=[[-1, 128]], channel_multiplier=1).then_inc(ident_built, 1)
            for n, k in enumerate(range(1 - GROUPS, GROUPS)):
                pool.wait_ge(fold_built, n + 1)
                pool.affine_select(out=fold[:, :], in_=fold[:, :], compare_op=ALU.not_equal,
                                   fill=-1.0 / (SIDE * SIDE), base=32 * k, pattern=[[-1, 128]],
                                   channel_multiplier=1).then_inc(fold_built, 1)
            pool.memset(raw[:, 1, :, :], 0.0).then_inc(filt_zeroed, 1)
            pool.memset(credit[:, 0:1], 0.0).then_inc(pair_ready, 6)
            pool.memset(credit[:, 1:2], 0.0).then_inc(final_added, PARTS)
            pool.wait_ge(hats, 1 + TAPS + 2 + 6)
            pool.wait_ge(weights_copied, 1)
            products(pool, 1).then_inc(products_by_pool, 1)

            def step(u, h, before, first=False, final=False):
                if h >= 2 or not first:
                    pool.wait_ge(stored[h % 2], LOAD * before)
                for k in range(PARTS - 1 if final else PARTS):
                    a, b = divmod(k, 2)
                    pool.wait_ge(pair_ready, 6 * u + 6 + 3 * a + b + 1)
                    pool.wait_ge(final_added, PARTS * u + k + 1)
                    add_image(pool, h, k).then_inc(image_added, 1)
                    pool.wait_ge(image_added, PARTS * u + k + 1)
                    pool.wait_ge(pair_ready, 6 * u + 6 + 3 * a + b + 2)
                    add_pair(pool, h, k).then_inc(final_added, 1)

            spread(pool, pieces[:by_pool], spread_by_pool)
            pool.wait_ge(spread_by_sync, (GROUPS * GROUPS - by_pool) * DMA)
            pool.wait_ge(spread_by_pool, by_pool * DMA)
            for i in (0, 2):
                turn(pool, i).then_inc(turned_by_pool, 1)
                pool.wait_ge(turned_by_pool, i // 2 + 1)
                sum_filters(pool, i).then_inc(filt_summed_by_pool, 1)
            for n in range(BY_DVE, NS):
                low_filter(pool, n).then_inc(wlo_by_pool, 1)
            for h in range(RING):
                step(h, h, h // 2, first=True)
            with pool.Fori(1, UNITS // RING - 1) as it:
                for h in range(RING):
                    step(it * RING + h, h, it * (RING // 2) + h // 2)
            for h in range(RING):
                u = UNITS - RING + h
                step(u, h, u // 2, final=u == UNITS - 1)

        @block.tensor
        def _(pe):
            pe.wait_ge(weights_loaded, DMA)
            pe.wait_ge(ident_built, 2)
            by_point = wnat[:, :, :].rearrange("o g (c k) -> o k (g c)", k=POINTS)
            for k in range(POINTS):
                last = pe.matmul(banks[0][:, k * CH:(k + 1) * CH],
                                 by_point[:, k, :],
                                 ident[0:CH, 0:CH], start=True, stop=True)
            last.then_inc(weights_turned, 1)
            pe.wait_ge(wmax_ready, 1)
            pe.matmul(banks[1][0:1, 0:CH], wmax[:, :], ident[0:CH, 0:CH], start=True, stop=True).then_inc(wmax_row, 1)
            pe.wait_ge(srow_step, 6)
            pe.wait_ge(ones_built, 1)
            pe.matmul(banks[2][:, 0:2], ones[:, :], srow[:, 2:4], start=True, stop=True).then_inc(scales_in_psum, 1)
            pe.wait_ge(fold_built, 2 * GROUPS)

            def mean(u):
                pe.wait_ge(sum_ready, u + 1)
                pe.wait_ge(negmean_ready, u)
                pe.matmul(mean_ps[:, 0:PER], fold[:, :], xsum[:, :], start=True, stop=True).then_inc(mean_in_psum, 1)

            def variance(u):
                pe.wait_ge(ssq_ready, u + 1)
                pe.wait_ge(var_ready, u)
                pe.matmul(var_ps[:, 0:PER], fold[:, :], ssq[:, :], start=True, stop=True).then_inc(var_in_psum, 1)

            def third_blocks(u, h, s, into):
                i, j = STREAMS[s]
                if s < PACKED:
                    pe.wait_ge(whi_packs, s // 3 + 1)
                    pe.wait_ge(wlo_packs, s // 3 + 1)
                    pe.wait_ge(packed_by_act, PACKED * u + s + 1)
                for w, n in ((0, 0), (0, 1), (1, 0)):
                    if s < PACKED:
                        pe.matmul(into[:, :, 0:BELOW, :], (whi_packed, wlo_packed)[w][:, i, j, :],
                                  packed[:, h, n, s, :, :, 0:QW], start=False, stop=False)
                    else:
                        pe.matmul(into[:, :, 0:BELOW, :], (whi, wlo)[w][:, i, j, 0, 0:128],
                                  (xhi, xlo)[n][:, h, s, :, 2:SLOTS, 0:QW], start=False, stop=False)

            def convolve(u, h, s):
                i, j = STREAMS[s]
                if s < BY_DVE:
                    pe.wait_ge(wlo_by_dve, s + 1)
                else:
                    pe.wait_ge(wlo_by_pool, s - BY_DVE + 1)
                pe.wait_ge(lo_ready, NS * u + s + 1)
                if s < BANKS:
                    pe.wait_ge(pair_ready, 6 * u + s + 1)
                else:
                    pe.wait_ge(middle_ready, 3 * u + s - BANKS + 1)
                into = banks[(NS * h + s) % BANKS][:, 0:N].rearrange("p (m n q) -> p m n q", m=PER, q=QW)
                order = [(q, t, n) for q in range(2 if s < PACKED else 1) for t in (0, -1) for n in range(3)]
                order = order[:2] + order[3:] + order[2:3]
                for c, (q, t, n) in enumerate(order):
                    if c == len(order) - 1:
                        third_blocks(u, h, s, into)
                    v = (1 - t) * GROUPS * CH
                    wide = min(QW, width(s) - q)
                    w, xs = ((whi, xhi), (whi, xlo), (wlo, xhi))[n]
                    last = pe.matmul(into[:, :, :, 0:wide], w[:, i, j, q, v:v + 128],
                                     xs[:, h, s, :, t + 1:t + 1 + ROWS, q:q + wide],
                                     start=c == 0, stop=c == len(order) - 1)
                last.then_inc(conv_done, 1)

            def step(u, h, stats):
                for s in range(NS):
                    if stats and s == 1:
                        mean(u + 2)
                    if stats and s == 6:
                        variance(u + 2)
                    convolve(u, h, s)

            mean(0)
            variance(0)
            mean(1)
            variance(1)
            with pe.Fori(0, UNITS // 2 - 1) as it:
                for h in range(2):
                    step(it * 2 + h, h, True)
            step(UNITS - 2, 0, False)
            step(UNITS - 1, 1, False)


def kernel(**inputs):
    import numpy as np
    import concourse.bacc as bacc
    from concourse.bass_utils import run_bass_kernel_spmd

    nc = bacc.Bacc("TRN2", target_bir_lowering=False, num_devices=1)
    arrays, args = {}, []
    for name in ("x", "L0_conv_weight", "L0_conv_P", "L0_conv_bias"):
        a = np.ascontiguousarray(inputs[name])
        arrays[name] = a
        args.append(nc.dram_tensor(name, a.shape, mybir.dt.from_np(a.dtype), kind="ExternalInput").ap())
    args.append(nc.dram_tensor("out", (BATCH, CH, SIDE, SIDE), mybir.dt.float32, kind="ExternalOutput").ap())
    build(nc, *args)
    r = run_bass_kernel_spmd(nc, [arrays], core_ids=[0])
    return r.results[0]["out"]
```

```python
import concourse.bass as bass
from concourse import mybir
from contextlib import ExitStack

BATCH, CH, SIDE = 32, 32, 56
TAPS = 7
POINTS = 9
GROUPS = 4
ROWS = SIDE // GROUPS
PER = 2
UNITS = BATCH // PER
LINES = PER * ROWS
PLANE = ROWS * SIDE
PAD = TAPS // 2
WPAD = 64
QW = SIDE // 4
QS = QW + 1
QP = 16
N = LINES * QW
SLOTS = ROWS + 1
XLINES = PER * SLOTS
BELOW = ROWS - 1
V = 12
HALF = 64
VO = V * CH
X_SCALE = 256.0
W_SCALE = 2048.0
EPS = 1e-5
RING = 4
BANKS = 6
STREAMS = [(1, 1), (1, 0), (1, 2), (0, 1), (0, 0), (0, 2), (2, 1), (2, 0), (2, 2)]
NS = len(STREAMS)
PACKED = NS - 1
BY_DVE = 3
PARTS = 4
STEP_OF = [4, 5, 5, 6, 7, 7, 6, 8, 8]
PREP = 8
NEWTON = 5
DMA = 16
LOAD = PER * GROUPS * DMA


def build(nc, x, weight, P, bias, out):
    fp32 = mybir.dt.float32
    fp16 = mybir.dt.float16
    i32 = mybir.dt.int32
    ALU = mybir.AluOpType
    ACT = mybir.ActivationFunctionType
    AX = mybir.AxisListType

    ctx = ExitStack()
    with ctx:
        def sb(name, shape, dt):
            return ctx.enter_context(nc.sbuf_tensor(name, shape, dt))

        def sem(name):
            return ctx.enter_context(nc.semaphore(name))

        xraw = sb("xraw", [128, RING * PER, PLANE], fp32)
        junk = sb("junk", [128, 2, PER, PLANE], fp16)
        xn = sb("xn", [128, XLINES, WPAD], fp32)
        d = sb("d", [128, 2, XLINES, WPAD // 2], fp32)
        e = sb("e", [128, 3, 2, XLINES, QP], fp32)
        xhi = sb("xhi", [128, 2, NS, PER, SLOTS, QP], fp16)
        xlo = sb("xlo", [128, 2, NS, PER, SLOTS, QP], fp16)
        packed = sb("packed", [128, 2, 2, PACKED, PER, BELOW, QP], fp16)
        late = sb("late", [128, 9 * N + PER * PLANE], fp32)
        middle = late[:, 0:3 * N].rearrange("p (j n) -> p j n", j=3)
        pair = late[:, 3 * N:9 * N].rearrange("p (j n) -> p j n", j=6)
        part = late[:, 9 * N:9 * N + 4 * N].rearrange("p (k n) -> p k n", k=4)
        prod = late[:, 0:2 * TAPS * CH * POINTS].rearrange("p (a o k) -> p a o k", o=CH, k=POINTS)
        result = sb("result", [128, 2, PER * PLANE], fp32)
        fold = sb("fold", [128, 128], fp32)
        xsum = sb("xsum", [128, PER], fp32)
        negmean = sb("negmean", [128, PER], fp32)
        ssq = sb("ssq", [128, PER], fp32)
        var = sb("var", [128, PER], fp32)
        std = sb("std", [128, PER], fp32)
        rinv = sb("rinv", [128, PER], fp32)
        rtmp = sb("rtmp", [128, PER], fp32)
        scale = sb("scale", [128, PER], fp32)
        ident = sb("ident", [128, 128], fp32)
        ones = sb("ones", [1, 128], fp32)
        pts = sb("pts", [128, 2, POINTS], fp32)
        setup0 = packed[:, 0, :, :, :, :, :].rearrange("p a s m n q -> p (a s m n q)").bitcast(fp32)
        setup1 = packed[:, 1, :, :, :, :, :].rearrange("p a s m n q -> p (a s m n q)").bitcast(fp32)
        wnat = setup0[0:CH, 0:GROUPS * CH * POINTS].rearrange("p (g w) -> p g w", g=GROUPS)
        coloff = sb("coloff", [128, 2], fp32)
        wts = sb("wts", [128, POINTS, CH], fp32)
        hath = sb("hath", [128, TAPS, POINTS], fp32)
        hatw = sb("hatw", [128, 2, POINTS], fp32)
        hat2 = sb("hat2", [128, 2, TAPS, POINTS], fp32)
        kern = sb("kern", [128, 2, TAPS * CH], fp32)
        raw = result[:, :, :].rearrange("p a n -> p (a n)")[:, 0:8 * VO].rearrange("p (i q v) -> p i q v", i=2, q=4)
        outer = setup1[:, 0:8 * VO].rearrange("p (i q v) -> p i q v", i=2, q=4)
        inner = sb("inner", [128, 4, VO], fp32)
        filtsum = [late[:, a:a + 2 * VO].rearrange("p (q v) -> p q v", q=2) for a in (9 * N, 3 * N, 9 * N + 2 * VO)]
        whi = sb("whi", [128, 3, 3, 2, VO], fp16)
        wlo = sb("wlo", [128, 3, 3, 2, VO], fp16)
        whi_packed = sb("whi_packed", [128, 3, 3, 4 * CH], fp16)
        wlo_packed = sb("wlo_packed", [128, 3, 3, 4 * CH], fp16)
        wmax = sb("wmax", [CH, 1], fp32)
        srow = sb("srow", [1, 4], fp32)
        unused = sb("unused", [1, 1], fp32)
        credit = sb("credit", [1, 2], fp32)
        scales = sb("scales", [128, 2], fp32)
        biascol = sb("biascol", [128, 1], fp32)

        banks = [ctx.enter_context(nc.psum_tensor(f"bank{k}", [128, 512], fp32)) for k in range(BANKS)]
        mean_ps = ctx.enter_context(nc.psum_tensor("mean_ps", [128, 512], fp32))
        var_ps = ctx.enter_context(nc.psum_tensor("var_ps", [128, 512], fp32))

        x_loaded = [sem("x_loaded_even"), sem("x_loaded_odd")]
        stored = [sem("stored_even"), sem("stored_odd")]
        points_loaded = sem("points_loaded")
        weights_loaded = sem("weights_loaded")
        weights_turned = sem("weights_turned")
        weights_copied = sem("weights_copied")
        bias_loaded = sem("bias_loaded")
        spread_by_sync = sem("spread_by_sync")
        spread_by_pool = sem("spread_by_pool")
        sum_ready = sem("sum_ready")
        mean_in_psum = sem("mean_in_psum")
        negmean_ready = sem("negmean_ready")
        ssq_ready = sem("ssq_ready")
        var_in_psum = sem("var_in_psum")
        var_ready = sem("var_ready")
        std_ready = sem("std_ready")
        newton = sem("newton")
        prepared = sem("prepared")
        hi_ready = sem("hi_ready")
        lo_ready = sem("lo_ready")
        packed_by_act = sem("packed_by_act")
        packed_by_dve = sem("packed_by_dve")
        conv_done = sem("conv_done")
        middle_ready = sem("middle_ready")
        pair_ready = sem("pair_ready")
        image_added = sem("image_added")
        last_image_added = sem("last_image_added")
        final_added = sem("final_added")
        fold_built = sem("fold_built")
        ident_built = sem("ident_built")
        ones_built = sem("ones_built")
        coloff_built = sem("coloff_built")
        filt_zeroed = sem("filt_zeroed")
        xn_zeroed = sem("xn_zeroed")
        hats = sem("hats")
        wmax_ready = sem("wmax_ready")
        wmax_row = sem("wmax_row")
        srow_step = sem("srow_step")
        scales_in_psum = sem("scales_in_psum")
        scales_ready = sem("scales_ready")
        kern_ready = sem("kern_ready")
        filt_summed = sem("filt_summed")
        whi_ready = sem("whi_ready")
        wlo_by_dve = sem("wlo_by_dve")
        wlo_by_pool = sem("wlo_by_pool")
        filt_summed_by_pool = sem("filt_summed_by_pool")
        products_by_pool = sem("products_by_pool")
        turned_by_act = sem("turned_by_act")
        turned_by_dve = sem("turned_by_dve")
        filter_packed = sem("filter_packed")
        edges_zeroed = sem("edges_zeroed")

        block = ctx.enter_context(nc.Block())

        def image(r, m):
            return xraw[:, r * PER + m, :]

        def dram_rows(t, u, m, g):
            return t[bass.ds(u * PER + m, 1), :, (g + 1) % GROUPS::GROUPS, :].rearrange("m c n w -> (m c) n w")

        BATCHES = [(0, 1), (1, 2), (3, 1), (4, 2), (6, 1), (7, 2)]

        def stream(s):
            i, j = STREAMS[s]
            if j != 1:
                return e[:, i, :, :, 0:QS]
            if i == 1:
                return xn[:, :, 3:4 * width(s):4]
            return d[:, i // 2, :, 1:2 * width(s):2]

        def width(s):
            return QS - 1 if STREAMS[s] in ((1, 1), (1, 2), (2, 1), (2, 2)) else QS

        def halves(t, par, s, count):
            wide = width(s) if count == 1 else QS
            return t[:, par, s:s + count, :, :, 0:wide].rearrange(
                "p s m n q -> p (s m n) q" if count == 1 else "p s m n q -> p s (m n) q", s=count)

        def both(ap, step):
            return bass.AP(tensor=ap.tensor, offset=ap.offset, ap=[ap.ap[0], [step, 2], *ap.ap[1:]])

        def filter_of(i, j):
            return filtsum[i] if j == 1 else level_one(i, j // 2)

        def level_one(i, m):
            return inner[:, m::2, :] if i == 1 else outer[:, i // 2, m::2, :]

        TURNS = [((1, 4), (0, 3)), ((0, 1), (3, 4))]

        def phases(ap, a, b):
            return ap.rearrange("p q (r v) -> p q r v", v=GROUPS * CH)[:, :, :, a * CH:b * CH]

        def turn(copy, i):
            for (a, b), (c, f) in TURNS:
                last = copy(phases(outer[:, i // 2, :, :], c, f), phases(raw[:, i // 2, :, :], a, b))
            return last

        def add_turned(eng, o, x, y):
            for (a, b), (c, f) in TURNS:
                last = eng.tensor_tensor(phases(o, c, f), phases(x, a, b), phases(y, a, b), ALU.add)
            return last

        def pack_images(op, half, par, which, s0, s1):
            src = (xhi, xlo)[which]
            return op(packed[HALF * half:HALF * (half + 1), par, which, s0:s1, :, :, 0:QW].rearrange(
                          "p s m n q -> p (s m) n q"),
                      src[0:HALF, par, s0:s1, :, 2:SLOTS, half:half + QW].rearrange("p s m n q -> p (s m) n q"))

        def pack_filter(op, dst, src, s):
            i, j = STREAMS[s]
            for half in range(2):
                last = op(dst[HALF * half:HALF * (half + 1), i, j, :], src[0:HALF, i, j, half, 0:GROUPS * CH])
            return last

        def spread(queue, pieces, done):
            queue.wait_ge(filt_zeroed, 2)
            queue.wait_ge(kern_ready, 1)
            for g, q in pieces:
                queue.dma_start(raw[32 * g:32 * g + 32, :, q, (g + 2) * CH:(g + 2 + TAPS) * CH],
                                kern[32 * q:32 * q + 32, :, :]).then_inc(done, DMA)

        pieces = [(g, q) for g in range(GROUPS) for q in range(GROUPS)]
        by_pool = 6

        def cols(t, k):
            return t.rearrange("p (l q k) -> p l q k", q=QW, k=4)[:, :, :, k]

        def lines(ap):
            return ap.rearrange("p (l q) -> p l q", q=QW)

        def add_image(eng, h, k):
            photo = xraw[:, PER * h:PER * (h + 1), :].rearrange("p m n -> p (m n)")
            return eng.tensor_tensor(lines(part[:, k, :]), lines(pair[:, 3 * (k // 2), :]),
                                     cols(photo, 2 * (k % 2) + k // 2), ALU.add)

        def add_pair(eng, h, k):
            return eng.tensor_tensor(cols(result[:, h % 2, :], 2 * (k % 2) + k // 2), lines(part[:, k, :]),
                                     lines(pair[:, 3 * (k // 2) + 1 + k % 2, :]), ALU.add)

        def products(eng, a):
            return eng.tensor_tensor(prod[:, TAPS * a:TAPS * (a + 1), :, :],
                                     hat2[:, a, :, :].unsqueeze(2).broadcast_to([128, TAPS, CH, POINTS]),
                                     wts[:, :, :].rearrange("p k o -> p o k").unsqueeze(1).broadcast_to(
                                         [128, TAPS, CH, POINTS]), ALU.mult)

        def low_filter(eng, n):
            i, j = STREAMS[n]
            eng.wait_ge(whi_ready, n + 1)
            return eng.tensor_tensor(wlo[:, i, j, :, :], filter_of(i, j), whi[:, i, j, :, :], ALU.subtract)

        @block.sync
        def _(sp):
            def load(u, r):
                for m in range(PER):
                    for g in range(GROUPS):
                        sp.dma_start(image(r, m)[32 * g:32 * g + 32, :].rearrange("c (n w) -> c n w", w=SIDE),
                                     dram_rows(x, u, m, g)).then_inc(x_loaded[r % 2], DMA)

            def finished(u):
                sp.wait_ge(final_added, PARTS * u + 2 * PARTS)

            def store(u, par):
                for m in range(PER):
                    for g in range(GROUPS):
                        sp.dma_start(dram_rows(out, u, m, g),
                                     result[32 * g:32 * g + 32, par, PLANE * m:PLANE * (m + 1)].rearrange(
                                         "c (n w) -> c n w", w=SIDE)).then_inc(stored[par], DMA)

            sp.dma_start(wnat[:, :, :], weight.rearrange("o (a c) k -> o a (c k)", a=1)
                          .broadcast_to([CH, GROUPS, CH * POINTS])).then_inc(weights_loaded, DMA)
            for t in range(2):
                sp.dma_start(pts[:, t, :], P[t:t + 1, :, :].broadcast_to([GROUPS, CH, POINTS])
                              ).then_inc(points_loaded, DMA)
            load(0, 0)
            load(1, 1)
            sp.dma_start(biascol[:, :], bias.rearrange("(a c b) -> a c b", a=1, b=1)
                          .broadcast_to([GROUPS, CH, 1])).then_inc(bias_loaded, DMA)
            spread(sp, pieces[by_pool:], spread_by_sync)
            sp.wait_ge(sum_ready, 1)
            load(2, 2)
            sp.wait_ge(sum_ready, 2)
            load(3, 3)
            with sp.Fori(0, UNITS // RING - 1) as it:
                for h in range(RING):
                    u = it * RING + h
                    finished(u)
                    store(u, h % 2)
                    sp.wait_ge(sum_ready, u + 3)
                    load(u + RING, h)
            for u in range(UNITS - RING, UNITS):
                finished(u)
                store(u, u % 2)
            for par in range(2):
                sp.wait_ge(stored[par], LOAD * (UNITS // 2))

        @block.scalar
        def _(act):
            act.wait_ge(ones_built, 1)
            act.activation(unused[:, :], ones[:, 0:1], ACT.Sqrt)

            def sums(u, r, nth):
                act.wait_ge(x_loaded[r % 2], LOAD * (nth + 1))
                act.wait_ge(mean_in_psum, u)
                for m in range(PER):
                    last = act.activation(junk[:, r % 2, m, :], image(r, m), ACT.Identity, accum_out=xsum[:, m:m + 1])
                last.then_inc(sum_ready, 1)

            def squares(u, r):
                act.wait_ge(negmean_ready, u + 1)
                for m in range(PER):
                    last = act.activation(junk[:, r % 2, m, :], image(r, m), ACT.Square, bias=negmean[:, m:m + 1],
                                          accum_out=ssq[:, m:m + 1])
                last.then_inc(ssq_ready, 1)

            def root(u):
                act.wait_ge(var_ready, u + 1)
                act.activation(std[:, :], var[:, :], ACT.Sqrt).then_inc(std_ready, 1)

            def high(u, par, s, count):
                act.wait_ge(prepared, PREP * u + STEP_OF[s])
                act.activation(halves(xhi, par, s, count), stream(s), ACT.Copy).then_inc(hi_ready, count)

            def copy(o, i):
                return act.activation(o, i, ACT.Copy)

            def pack(u, par, s0, s1):
                act.wait_ge(hi_ready, NS * u + s1)
                act.wait_ge(lo_ready, NS * u + 1)
                if not (isinstance(u, int) and u < 2):
                    pack_images(copy, 0, par, 0, s0, s1)
                pack_images(copy, 1, par, 0, s0, s1)
                act.wait_ge(lo_ready, NS * u + s1)
                pack_images(copy, 1, par, 1, s0, s1).then_inc(packed_by_act, s1 - s0)

            def step(u, h, nth, streams, stats, early):
                def mid(j):
                    act.wait_ge(conv_done, NS * u + j + 1)
                    act.wait_ge(pair_ready, 6 * u + 4 + j)
                    act.activation(middle[:, j, :], banks[(NS * h + j) % BANKS][:, 0:N], ACT.Identity,
                                   bias=biascol[:, 0:1] if STREAMS[j] == (1, 1) else 0.0,
                                   scale=scales[:, 1:2]).then_inc(middle_ready, 1)
                for j in range(3):
                    mid(j)
                    if streams:
                        for batch in BATCHES[2 * j:2 * j + 2]:
                            high(u + 1, 1 - h % 2, *batch)
                    if stats and j == 0:
                        squares(u + 2, (h + 2) % RING)
                if streams:
                    pack(u + 1, 1 - h % 2, 0, PACKED)
                if early:
                    sums(u + 3, (h + 3) % RING, nth)
                if stats:
                    root(u + 2)

            act.wait_ge(weights_turned, 1)
            act.activation(wts[:, :, :], banks[0][:, 0:POINTS * CH].rearrange("p (k o) -> p k o", o=CH), ACT.Copy
                           ).then_inc(weights_copied, 1)
            sums(0, 0, 0)
            squares(0, 0)
            root(0)
            sums(1, 1, 0)
            high(0, 0, *BATCHES[0])
            high(0, 0, *BATCHES[1])
            squares(1, 1)
            act.wait_ge(spread_by_sync, (GROUPS * GROUPS - by_pool) * DMA)
            act.wait_ge(spread_by_pool, by_pool * DMA)
            turn(copy, 0).then_inc(turned_by_act, 1)
            for n, (i, j) in enumerate(STREAMS):
                if n == 3:
                    sums(2, 2, 1)
                if j == 1:
                    if i == 1:
                        act.wait_ge(filt_summed, 2)
                    else:
                        act.wait_ge(filt_summed_by_pool, {0: 2, 2: 3}[i])
                elif i == 1:
                    act.wait_ge({0: filt_summed, 2: filt_summed_by_pool}[j], 1)
                else:
                    act.wait_ge({0: turned_by_act, 2: turned_by_dve}[i], 1)
                copy(whi[:, i, j, :, :], filter_of(i, j)).then_inc(whi_ready, 1)
                if n == 1:
                    high(0, 0, *BATCHES[2])
                    high(0, 0, *BATCHES[3])
                if n == 3:
                    root(1)
                if n == 4:
                    high(0, 0, *BATCHES[4])
                    high(0, 0, *BATCHES[5])
            pack(0, 0, 6, PACKED)
            act.wait_ge(bias_loaded, DMA)
            for h in range(RING):
                step(h, h, (h + 3) // 2, True, True, True)
            with act.Fori(1, UNITS // RING - 1) as it:
                for h in range(RING):
                    step(it * RING + h, h, it * (RING // 2) + (h + 3) // 2, True, True, True)
            for h in range(RING):
                u = UNITS - RING + h
                step(u, h, (u + 3) // 2, u + 1 < UNITS, u + 2 < UNITS, u + 3 < UNITS)

        @block.vector
        def _(dve):
            def mean(u):
                dve.wait_ge(mean_in_psum, u + 1)
                dve.tensor_copy(negmean[:, :], mean_ps[:, 0:PER]).then_inc(negmean_ready, 1)

            def rstd(u):
                dve.wait_ge(var_in_psum, u + 1)
                dve.tensor_scalar(var[:, :], var_ps[:, 0:PER], -1.0, EPS, ALU.mult, ALU.add).then_inc(var_ready, 1)
                dve.wait_ge(std_ready, u + 1)
                k = NEWTON * u
                dve.reciprocal(rinv[:, :], std[:, :]).then_inc(newton, 1)
                dve.wait_ge(newton, k + 1)
                dve.tensor_tensor(rtmp[:, :], rinv[:, :], rinv[:, :], ALU.mult).then_inc(newton, 1)
                dve.wait_ge(newton, k + 2)
                dve.tensor_tensor(rtmp[:, :], rtmp[:, :], var[:, :], ALU.mult).then_inc(newton, 1)
                dve.wait_ge(newton, k + 3)
                dve.tensor_scalar(rtmp[:, :], rtmp[:, :], -0.5 * X_SCALE, 1.5 * X_SCALE,
                                  ALU.mult, ALU.add).then_inc(newton, 1)
                dve.wait_ge(newton, k + 4)
                dve.tensor_tensor(scale[:, :], rtmp[:, :], rinv[:, :], ALU.mult).then_inc(newton, 1)

            def normalise(u, r):
                dve.wait_ge(newton, NEWTON * (u + 1))
                if not isinstance(u, int) or u > 0:
                    dve.wait_ge(hi_ready, NS * u)
                    dve.wait_ge(lo_ready, NS * u)
                for m in range(PER):
                    for a, b, slot in ((0, 96, 1), (96, 128, 0)):
                        line = SLOTS * m + slot
                        dve.tensor_scalar(xn[a:b, line:line + ROWS, PAD:PAD + SIDE],
                                          image(r, m)[a:b, :].rearrange("p (n w) -> p n w", w=SIDE),
                                          negmean[a:b, m:m + 1], scale[a:b, m:m + 1],
                                          ALU.add, ALU.mult).then_inc(prepared, 1)

            def differences(u, steps):
                def less(step, o, x0, shift, x1, need):
                    if step in steps:
                        dve.wait_ge(prepared, PREP * u + need)
                        dve.tensor_tensor(o, both(x0, shift), both(x1, 0), ALU.subtract).then_inc(prepared, 1)
                half = 2 * QS + 1
                less(5, e[:, 1, :, :, 0:QS], xn[:, :, 1:4 * QS + 1:4], 4, xn[:, :, 3:4 * QS:4], 4)
                less(6, d[:, :, :, 0:half], xn[:, :, 0:2 * half:2], 2, xn[:, :, 1:2 * half:2], 4)
                for i in (0, 2):
                    less(7 + i // 2, e[:, i, :, :, 0:QS], d[:, i // 2, :, 0:2 * QS:2], 2,
                         d[:, i // 2, :, 1:2 * QS:2], 6)

            def low(u, par, s, count):
                dve.wait_ge(hi_ready, NS * u + s + count)
                dve.tensor_tensor(halves(xlo, par, s, count), stream(s), halves(xhi, par, s, count),
                                  ALU.subtract).then_inc(lo_ready, count)

            def pairs(u, h, s):
                dve.wait_ge(conv_done, NS * u + s + 1)
                if s == 3:
                    dve.wait_ge(final_added, PARTS * u + PARTS)
                dve.wait_ge(middle_ready, 3 * u + s % 3 + 1)
                dve.scalar_tensor_tensor(pair[:, s - 3, :], banks[(NS * h + s) % BANKS][:, 0:N], scales[:, 1:2],
                                         middle[:, s % 3, :], ALU.mult, ALU.add).then_inc(pair_ready, 1)

            def pack(u, par, s0, s1, everything=False):
                dve.wait_ge(lo_ready, NS * u + s1)
                if isinstance(u, int) and u < 2:
                    pack_images(dve.tensor_copy, 0, par, 0, s0, s1)
                pack_images(dve.tensor_copy, 0, par, 1, s0, s1).then_inc(packed_by_dve, s1 - s0)
                if everything:
                    pack_images(dve.tensor_copy, 1, par, 0, s0, s1)
                    pack_images(dve.tensor_copy, 1, par, 1, s0, s1).then_inc(packed_by_act, s1 - s0)

            def filters(s0, s1):
                for s in range(s0, s1):
                    dve.wait_ge(wlo_by_pool, s - BY_DVE + 1)
                    pack_filter(dve.tensor_copy, whi_packed, whi, s)
                    pack_filter(dve.tensor_copy, wlo_packed, wlo, s).then_inc(filter_packed, 1)

            def step(u, h, streams, stats):
                if isinstance(u, int) and u == 0:
                    filters(4, 6)
                if streams:
                    normalise(u + 1, (h + 1) % RING)
                    differences(u + 1, (5,))
                if stats:
                    mean(u + 2)
                if streams:
                    if isinstance(u, int) and u == 0:
                        filters(6, PACKED)
                    differences(u + 1, range(6, PREP + 1))
                    if isinstance(u, int) and u == 0:
                        dve.wait_ge(wlo_by_pool, NS - BY_DVE)
                    for batch in BATCHES:
                        low(u + 1, 1 - h % 2, *batch)
                for s in range(3, 6):
                    pairs(u, h, s)
                if streams:
                    pack(u + 1, 1 - h % 2, 0, PACKED)
                for s in range(6, NS):
                    if stats and s == 8:
                        rstd(u + 2)
                    pairs(u, h, s)

            for g in range(GROUPS):
                for a in range(2):
                    dve.memset(coloff[32 * g:32 * g + 32, a:a + 1], -2.0 * g - a).then_inc(coloff_built, 1)
            dve.memset(ones[:, :], 1.0).then_inc(ones_built, 1)
            dve.memset(xn[:, :, 0:PAD], 0.0).then_inc(xn_zeroed, 1)
            dve.memset(xn[:, :, PAD + SIDE:WPAD], 0.0).then_inc(xn_zeroed, 1)
            dve.memset(xn[:, ::SLOTS, PAD:PAD + SIDE], 0.0).then_inc(xn_zeroed, 1)
            dve.memset(xn[96:128, ROWS::SLOTS, PAD:PAD + SIDE], 0.0).then_inc(xn_zeroed, 1)
            dve.memset(raw[:, 0, :, :], 0.0).then_inc(filt_zeroed, 1)
            dve.wait_ge(weights_loaded, DMA)
            dve.tensor_reduce(wmax[:, :], wnat[:, 0, :], AX.X, ALU.max, apply_absolute_value=True
                              ).then_inc(wmax_ready, 1)
            dve.wait_ge(points_loaded, 2 * DMA)
            dve.tensor_scalar(pts[:, :, :], pts[:, :, :], -float(PAD), float(PAD), ALU.max, ALU.min).then_inc(hats, 1)
            dve.wait_ge(hats, 1)
            dve.wait_ge(coloff_built, 2 * GROUPS)
            for r in range(TAPS):
                dve.tensor_scalar(hath[:, r, :], pts[:, 0, :], float(PAD), -float(TAPS - 1 - r),
                                  ALU.add, ALU.add).then_inc(hats, 1)
            for a in range(2):
                dve.tensor_scalar(hatw[:, a, :], pts[:, 1, :], float(PAD), coloff[:, a:a + 1],
                                  ALU.add, ALU.add).then_inc(hats, 1)
            k = 1 + TAPS + 2
            dve.wait_ge(hats, k)
            for t in (hath, hatw):
                dve.scalar_tensor_tensor(t[:, :, :], t[:, :, :], -1.0, t[:, :, :], ALU.mult, ALU.min).then_inc(hats, 1)
            dve.wait_ge(hats, k + 2)
            for t in (hath, hatw):
                dve.tensor_scalar(t[:, :, :], t[:, :, :], 1.0, 0.0, ALU.add, ALU.max).then_inc(hats, 1)
            dve.wait_ge(hats, k + 4)
            for a in range(2):
                dve.tensor_tensor(hat2[:, a, :, :], hath[:, :, :],
                                  hatw[:, a:a + 1, :].broadcast_to([128, TAPS, POINTS]), ALU.mult).then_inc(hats, 1)
            for t in (xhi, xlo):
                dve.memset(t[:, :, 0:PACKED, :, :, QS - 1:QS].rearrange("p a s m n q -> p a (s m n) q"),
                           0.0).then_inc(edges_zeroed, 1)
            dve.wait_ge(hats, k + 6)
            dve.wait_ge(weights_copied, 1)
            products(dve, 0).then_inc(hats, 1)
            dve.wait_ge(wmax_row, 1)
            dve.tensor_reduce(srow[:, 0:1], banks[1][0:1, 0:CH], AX.X, ALU.max).then_inc(srow_step, 1)
            dve.wait_ge(srow_step, 1)
            dve.tensor_scalar(srow[:, 1:2], srow[:, 0:1], 2.0 ** -80, None, ALU.max).then_inc(srow_step, 1)
            dve.wait_ge(srow_step, 2)
            dve.tensor_scalar(srow[:, 0:1].bitcast(i32), srow[:, 1:2].bitcast(i32), 0x7F800000, None,
                              ALU.bitwise_and).then_inc(srow_step, 1)
            dve.wait_ge(srow_step, 3)
            dve.reciprocal(srow[:, 1:2], srow[:, 0:1]).then_inc(srow_step, 1)
            dve.wait_ge(srow_step, 4)
            dve.tensor_scalar(srow[:, 2:3], srow[:, 1:2], W_SCALE, None, ALU.mult).then_inc(srow_step, 1)
            dve.tensor_scalar(srow[:, 3:4], srow[:, 0:1], 1.0 / (W_SCALE * X_SCALE), None,
                              ALU.mult).then_inc(srow_step, 1)
            dve.wait_ge(hats, k + 7)
            for a in range(2):
                if a:
                    mean(0)
                    dve.wait_ge(products_by_pool, 1)
                dve.tensor_reduce(kern[:, a, :].rearrange("p (r o) -> p r o", o=CH),
                                  prod[:, TAPS * a:TAPS * (a + 1), :, :], AX.X, ALU.add).then_inc(hats, 1)
            dve.wait_ge(scales_in_psum, 1)
            dve.tensor_copy(scales[:, :], banks[2][:, 0:2]).then_inc(scales_ready, 1)
            dve.wait_ge(scales_ready, 1)
            dve.wait_ge(hats, k + 9)
            dve.tensor_scalar(kern[:, :, :], kern[:, :, :], scales[:, 0:1], None, ALU.mult).then_inc(kern_ready, 1)
            rstd(0)
            dve.wait_ge(xn_zeroed, 4)
            normalise(0, 0)
            differences(0, (5,))
            mean(1)
            differences(0, (6, 7))
            dve.wait_ge(spread_by_sync, (GROUPS * GROUPS - by_pool) * DMA)
            dve.wait_ge(spread_by_pool, by_pool * DMA)
            dve.wait_ge(edges_zeroed, 2)
            add_turned(dve, level_one(1, 0), raw[:, 0, 0::2, :], raw[:, 1, 0::2, :]).then_inc(filt_summed, 1)
            low(0, 0, 0, 1)
            low(0, 0, 1, 2)
            dve.wait_ge(filt_summed, 1)
            dve.wait_ge(filt_summed_by_pool, 1)
            dve.tensor_tensor(filtsum[1], level_one(1, 0), level_one(1, 1), ALU.add).then_inc(filt_summed, 1)
            pack(0, 0, 0, 3, everything=True)
            for n in range(BY_DVE):
                low_filter(dve, n).then_inc(wlo_by_dve, 1)
                pack_filter(dve.tensor_copy, whi_packed, whi, n)
                dve.wait_ge(wlo_by_dve, n + 1)
                pack_filter(dve.tensor_copy, wlo_packed, wlo, n).then_inc(filter_packed, 1)
            turn(dve.tensor_copy, 2).then_inc(turned_by_dve, 1)
            differences(0, (8,))
            low(0, 0, 3, 1)
            low(0, 0, 4, 2)
            pack(0, 0, 3, 6, everything=True)
            rstd(1)
            filters(3, 4)
            low(0, 0, 6, 1)
            low(0, 0, 7, 2)
            pack(0, 0, 6, PACKED)
            for h in range(RING):
                step(h, h, True, True)
            with dve.Fori(1, UNITS // RING - 1) as it:
                for h in range(RING):
                    step(it * RING + h, h, True, True)
            for h in range(RING):
                u = UNITS - RING + h
                step(u, h, u + 1 < UNITS, u + 2 < UNITS)
            k = PARTS - 1
            dve.wait_ge(pair_ready, 6 * UNITS + 4)
            dve.wait_ge(final_added, PARTS * (UNITS - 1) + PARTS)
            add_image(dve, RING - 1, k).then_inc(last_image_added, 1)
            dve.wait_ge(pair_ready, 6 * UNITS + 6)
            dve.wait_ge(stored[1], LOAD * (UNITS // 2 - 1))
            dve.wait_ge(final_added, PARTS * UNITS + k)
            dve.wait_ge(last_image_added, 1)
            add_pair(dve, RING - 1, k).then_inc(final_added, 1)

        @block.gpsimd
        def _(pool):
            pool.memset(ident[:, :], 0.0).then_inc(ident_built, 1)
            pool.memset(fold[:, :], 0.0).then_inc(fold_built, 1)
            pool.wait_ge(ident_built, 1)
            pool.affine_select(out=ident[:, :], in_=ident[:, :], compare_op=ALU.not_equal, fill=1.0,
                               base=0, pattern=[[-1, 128]], channel_multiplier=1).then_inc(ident_built, 1)
            for n, k in enumerate(range(1 - GROUPS, GROUPS)):
                pool.wait_ge(fold_built, n + 1)
                pool.affine_select(out=fold[:, :], in_=fold[:, :], compare_op=ALU.not_equal,
                                   fill=-1.0 / (SIDE * SIDE), base=32 * k, pattern=[[-1, 128]],
                                   channel_multiplier=1).then_inc(fold_built, 1)
            pool.memset(raw[:, 1, :, :], 0.0).then_inc(filt_zeroed, 1)
            pool.memset(credit[:, 0:1], 0.0).then_inc(pair_ready, 6)
            pool.memset(credit[:, 1:2], 0.0).then_inc(final_added, PARTS)
            pool.wait_ge(hats, 1 + TAPS + 2 + 6)
            pool.wait_ge(weights_copied, 1)
            products(pool, 1).then_inc(products_by_pool, 1)

            def step(u, h, before, first=False, final=False):
                if h >= 2 or not first:
                    pool.wait_ge(stored[h % 2], LOAD * before)
                for k in range(PARTS - 1 if final else PARTS):
                    a, b = divmod(k, 2)
                    pool.wait_ge(pair_ready, 6 * u + 6 + 3 * a + 1)
                    pool.wait_ge(final_added, PARTS * u + k + 1)
                    add_image(pool, h, k).then_inc(image_added, 1)
                    pool.wait_ge(image_added, PARTS * u + k + 1)
                    pool.wait_ge(pair_ready, 6 * u + 6 + 3 * a + b + 2)
                    add_pair(pool, h, k).then_inc(final_added, 1)

            spread(pool, pieces[:by_pool], spread_by_pool)
            pool.wait_ge(spread_by_sync, (GROUPS * GROUPS - by_pool) * DMA)
            pool.wait_ge(spread_by_pool, by_pool * DMA)
            add_turned(pool, level_one(1, 1), raw[:, 0, 1::2, :], raw[:, 1, 1::2, :]).then_inc(filt_summed_by_pool, 1)
            for i in (0, 2):
                add_turned(pool, filtsum[i], raw[:, i // 2, 0::2, :], raw[:, i // 2, 1::2, :]
                           ).then_inc(filt_summed_by_pool, 1)
            for n in range(BY_DVE, NS):
                low_filter(pool, n).then_inc(wlo_by_pool, 1)
            for h in range(RING):
                step(h, h, h // 2, first=True)
            with pool.Fori(1, UNITS // RING - 1) as it:
                for h in range(RING):
                    step(it * RING + h, h, it * (RING // 2) + h // 2)
            for h in range(RING):
                u = UNITS - RING + h
                step(u, h, u // 2, final=u == UNITS - 1)

        @block.tensor
        def _(pe):
            pe.wait_ge(weights_loaded, DMA)
            pe.wait_ge(ident_built, 2)
            by_point = wnat[:, :, :].rearrange("o g (c k) -> o k (g c)", k=POINTS)
            for k in range(POINTS):
                last = pe.matmul(banks[0][:, k * CH:(k + 1) * CH],
                                 by_point[:, k, :],
                                 ident[0:CH, 0:CH], start=True, stop=True)
            last.then_inc(weights_turned, 1)
            pe.wait_ge(wmax_ready, 1)
            pe.matmul(banks[1][0:1, 0:CH], wmax[:, :], ident[0:CH, 0:CH], start=True, stop=True).then_inc(wmax_row, 1)
            pe.wait_ge(srow_step, 6)
            pe.wait_ge(ones_built, 1)
            pe.matmul(banks[2][:, 0:2], ones[:, :], srow[:, 2:4], start=True, stop=True).then_inc(scales_in_psum, 1)
            pe.wait_ge(fold_built, 2 * GROUPS)

            def mean(u):
                pe.wait_ge(sum_ready, u + 1)
                pe.wait_ge(negmean_ready, u)
                pe.matmul(mean_ps[:, 0:PER], fold[:, :], xsum[:, :], start=True, stop=True).then_inc(mean_in_psum, 1)

            def variance(u):
                pe.wait_ge(ssq_ready, u + 1)
                pe.wait_ge(var_ready, u)
                pe.matmul(var_ps[:, 0:PER], fold[:, :], ssq[:, :], start=True, stop=True).then_inc(var_in_psum, 1)

            def third_blocks(u, h, s, into):
                i, j = STREAMS[s]
                if s < PACKED:
                    pe.wait_ge(filter_packed, s + 1)
                    pe.wait_ge(packed_by_dve, PACKED * u + s + 1)
                    pe.wait_ge(packed_by_act, PACKED * u + s + 1)
                for w, n in ((0, 0), (0, 1), (1, 0)):
                    if s < PACKED:
                        pe.matmul(into[:, :, 0:BELOW, :], (whi_packed, wlo_packed)[w][:, i, j, :],
                                  packed[:, h, n, s, :, :, 0:QW], start=False, stop=False)
                    else:
                        pe.matmul(into[:, :, 0:BELOW, :], (whi, wlo)[w][:, i, j, 0, 0:128],
                                  (xhi, xlo)[n][:, h, s, :, 2:SLOTS, 0:QW], start=False, stop=False)

            def convolve(u, h, s):
                i, j = STREAMS[s]
                pe.wait_ge(whi_ready, s + 1)
                pe.wait_ge(lo_ready, NS * u + s + 1)
                if s < BANKS:
                    pe.wait_ge(pair_ready, 6 * u + s + 1)
                else:
                    pe.wait_ge(middle_ready, 3 * u + s - BANKS + 1)
                into = banks[(NS * h + s) % BANKS][:, 0:N].rearrange("p (m n q) -> p m n q", m=PER, q=QW)
                order = [(q, t, n) for n in range(3) for q in range(2 if s < PACKED else 1) for t in (0, -1)]
                order = [c for c in order if c != (0, 0, 2)] + [(0, 0, 2)]
                for c, (q, t, n) in enumerate(order):
                    if n == 2 and order[c - 1][2] == 1:
                        if s < BY_DVE:
                            pe.wait_ge(wlo_by_dve, s + 1)
                        else:
                            pe.wait_ge(wlo_by_pool, s - BY_DVE + 1)
                    if c == len(order) - 1:
                        third_blocks(u, h, s, into)
                    v = (1 - t) * GROUPS * CH
                    wide = min(QW, width(s) - q)
                    w, xs = ((whi, xhi), (whi, xlo), (wlo, xhi))[n]
                    last = pe.matmul(into[:, :, :, 0:wide], w[:, i, j, q, v:v + 128],
                                     xs[:, h, s, :, t + 1:t + 1 + ROWS, q:q + wide],
                                     start=c == 0, stop=c == len(order) - 1)
                last.then_inc(conv_done, 1)

            def step(u, h, stats):
                for s in range(NS):
                    if stats and s == 1:
                        mean(u + 2)
                    if stats and s == 8:
                        variance(u + 2)
                    convolve(u, h, s)

            mean(0)
            variance(0)
            mean(1)
            variance(1)
            with pe.Fori(0, UNITS // 2 - 1) as it:
                for h in range(2):
                    step(it * 2 + h, h, True)
            step(UNITS - 2, 0, False)
            step(UNITS - 1, 1, False)


def kernel(**inputs):
    import numpy as np
    import concourse.bacc as bacc
    from concourse.bass_utils import run_bass_kernel_spmd

    nc = bacc.Bacc("TRN2", target_bir_lowering=False, num_devices=1)
    arrays, args = {}, []
    for name in ("x", "L0_conv_weight", "L0_conv_P", "L0_conv_bias"):
        a = np.ascontiguousarray(inputs[name])
        arrays[name] = a
        args.append(nc.dram_tensor(name, a.shape, mybir.dt.from_np(a.dtype), kind="ExternalInput").ap())
    args.append(nc.dram_tensor("out", (BATCH, CH, SIDE, SIDE), mybir.dt.float32, kind="ExternalOutput").ap())
    build(nc, *args)
    r = run_bass_kernel_spmd(nc, [arrays], core_ids=[0])
    return r.results[0]["out"]
```
